# Optimizing a Trainium2 kernel written in Bass

```python
import numpy as np
import jax
import jax.numpy as jnp

def _softmax(x, axis=-1):
    return jax.nn.softmax(x, axis=axis)

def _gelu(x):
    return jax.nn.gelu(x, approximate=True)

def _silu(x):
    return jax.nn.silu(x)

def _sigmoid(x):
    return jax.nn.sigmoid(x)

def _layernorm(x, axis=-1, eps=1e-05):
    m = jnp.mean(x, axis=axis, keepdims=True)
    v = jnp.var(x, axis=axis, keepdims=True)
    return (x - m) / jnp.sqrt(v + eps)

def _scatter_add(tgt, idx, src, axis=0):
    return tgt.at[idx].add(src)

def _segment_sum(src, seg, n):
    return jax.ops.segment_sum(src, seg, n)
kernel_name = 'mk_xattn_ffn_d1_seqx_r4_3669d0'

def setup_inputs(seed: int=0):
    np.random.seed(seed)
    _w = jnp.asarray

    def _rec_inputs():
        import jax
        import jax.numpy as jnp
        _rk = jax.random.key(seed)
        x = -0.000125 + 0.9999 * jax.random.normal(jax.random.fold_in(_rk, 1), (2, 512, 1024), jnp.float32)
        _lenS = 512 - jax.random.randint(jax.random.fold_in(_rk, 7), (2,), 0, max(1, 512 // 4) + 1, jnp.int32)
        _lenS2 = 1024 - jax.random.randint(jax.random.fold_in(_rk, 8), (2,), 0, max(1, 1024 // 4) + 1, jnp.int32)
        _ctx_4096P = jax.random.normal(jax.random.fold_in(_rk, 11), (2, 16, 1024), jnp.float32)
        _ctx_4096c = jax.random.dirichlet(jax.random.fold_in(_rk, 511), 0.3 * jnp.ones((16,), jnp.float32), (2, 1024))
        _ctx_4096t = jnp.einsum('bsk,bkd->bsd', _ctx_4096c, _ctx_4096P)
        _ctx_4096t = _ctx_4096t * jax.lax.rsqrt(jnp.mean(jnp.square(_ctx_4096t)) + 1e-12) * 0.953939
        ctx_4096 = -5.72187e-05 + 0.999849 * (_ctx_4096t + 0.3 * jax.random.normal(jax.random.fold_in(_rk, 611), (2, 1024, 1024), jnp.float32))
        return (x, ctx_4096)
    x, ctx_4096 = _rec_inputs()

    def _L0_xattn_setup():
        import jax, jax.numpy as jnp
        import numpy as np
        QMIN = 0.0
        QMAX = 255.0

        def fake_quant(x, scale, zp):
            s = scale.reshape(())
            z = zp.reshape(())
            q = jnp.clip(jnp.round(x / s + z), QMIN, QMAX)
            return (q - z) * s
        key = jax.random.key(seed)
        k1, k2 = jax.random.split(key)
        B, M, K, N = (4, 512, 1024, 1024)
        x1 = jax.random.normal(k1, (B, M, K), dtype=jnp.float32)
        x2 = jax.random.normal(k2, (B, K, N), dtype=jnp.float32)
        x1_scale = jnp.full((1,), 8.0 / 255.0, dtype=jnp.float32)
        x1_zp = jnp.full((1,), 128.0, dtype=jnp.float32)
        x2_scale = jnp.full((1,), 8.0 / 255.0, dtype=jnp.float32)
        x2_zp = jnp.full((1,), 128.0, dtype=jnp.float32)
        return {'x1': x1, 'x2': x2, 'x1_scale': x1_scale, 'x1_zp': x1_zp, 'x2_scale': x2_scale, 'x2_zp': x2_zp}
    _L0_xattn_all = _L0_xattn_setup()
    _L0_xattn_in = {k: v for k, v in _L0_xattn_all.items() if k in ('x1_scale', 'x1_zp', 'x2_scale', 'x2_zp')}
    del _L0_xattn_all

    def _L0_ffn_setup():
        import jax, jax.numpy as jnp
        import numpy as np
        D_IN = 1024
        D_OUT = 1024
        RANK = 16
        NUM_EXPERTS = 8
        TOP_K = 2
        SCALING = 32.0 / RANK
        key = jax.random.key(seed)
        ks = jax.random.split(key, 6)
        x = jax.random.normal(ks[0], (4, 512, D_IN), dtype=jnp.float32)
        W_base = jax.random.normal(ks[1], (D_OUT, D_IN), dtype=jnp.float32) * (1.0 / np.sqrt(D_IN))
        b_base = jax.random.normal(ks[2], (D_OUT,), dtype=jnp.float32) * 0.01
        W_router = jax.random.normal(ks[3], (NUM_EXPERTS, D_IN), dtype=jnp.float32) * 0.01
        A_stack = jax.random.uniform(ks[4], (NUM_EXPERTS, RANK, D_IN), dtype=jnp.float32, minval=-1.0, maxval=1.0) * (1.0 / np.sqrt(D_IN))
        B_stack = jax.random.normal(ks[5], (NUM_EXPERTS, D_OUT, RANK), dtype=jnp.float32) * 0.02
        return {'x': x, 'W_base': W_base, 'b_base': b_base, 'W_router': W_router, 'A_stack': A_stack, 'B_stack': B_stack}
    _L0_ffn_all = _L0_ffn_setup()
    _L0_ffn_in = {k: v for k, v in _L0_ffn_all.items() if k in ('W_base', 'b_base', 'W_router', 'A_stack', 'B_stack')}
    del _L0_ffn_all
    return {'x': x, 'ctx_4096': ctx_4096, 'L0_xattn_x1_scale': _L0_xattn_in['x1_scale'], 'L0_xattn_x1_zp': _L0_xattn_in['x1_zp'], 'L0_xattn_x2_scale': _L0_xattn_in['x2_scale'], 'L0_xattn_x2_zp': _L0_xattn_in['x2_zp'], 'L0_ffn_W_base': _L0_ffn_in['W_base'], 'L0_ffn_b_base': _L0_ffn_in['b_base'], 'L0_ffn_W_router': _L0_ffn_in['W_router'], 'L0_ffn_A_stack': _L0_ffn_in['A_stack'], 'L0_ffn_B_stack': _L0_ffn_in['B_stack']}

def reference(x, ctx_4096, L0_xattn_x1_scale, L0_xattn_x1_zp, L0_xattn_x2_scale, L0_xattn_x2_zp, L0_ffn_W_base, L0_ffn_b_base, L0_ffn_W_router, L0_ffn_A_stack, L0_ffn_B_stack):
    import jax
    import jax.numpy as jnp

    def _L0_xattn_ref(x1, x2, x1_scale, x1_zp, x2_scale, x2_zp):
        import jax, jax.numpy as jnp
        import numpy as np
        QMIN = 0.0
        QMAX = 255.0

        def fake_quant(x, scale, zp):
            s = scale.reshape(())
            z = zp.reshape(())
            q = jnp.clip(jnp.round(x / s + z), QMIN, QMAX)
            return (q - z) * s
        q1 = fake_quant(x1, x1_scale, x1_zp)
        q2 = fake_quant(x2, x2_scale, x2_zp)
        return jnp.matmul(q1, q2)

    def _L0_ffn_ref(x, W_base, b_base, W_router, A_stack, B_stack):
        import jax, jax.numpy as jnp
        import numpy as np
        D_IN = 1024
        D_OUT = 1024
        RANK = 16
        NUM_EXPERTS = 8
        TOP_K = 2
        SCALING = 32.0 / RANK
        orig_shape = x.shape
        xf = x.reshape(-1, D_IN)
        logits = xf @ W_router.T
        probs = jax.nn.softmax(logits, axis=-1)
        topk_p, topk_i = jax.lax.top_k(probs, TOP_K)
        topk_p = topk_p / jnp.sum(topk_p, axis=-1, keepdims=True)
        combine = jnp.sum(jax.nn.one_hot(topk_i, NUM_EXPERTS, dtype=xf.dtype) * topk_p[..., None], axis=1)
        h = jnp.einsum('nd,erd->ner', xf, A_stack)
        h = h * combine[..., None]
        lora_out = jnp.einsum('ner,eor->no', h, B_stack) * SCALING
        base_out = xf @ W_base.T + b_base
        out = base_out + lora_out
        return out.reshape(orig_shape[:-1] + (D_OUT,))
    x = x + _L0_xattn_ref(_layernorm(x, axis=-1), ctx_4096, L0_xattn_x1_scale, L0_xattn_x1_zp, L0_xattn_x2_scale, L0_xattn_x2_zp)
    x = x + _L0_ffn_ref(_layernorm(x, axis=-1), L0_ffn_W_base, L0_ffn_b_base, L0_ffn_W_router, L0_ffn_A_stack, L0_ffn_B_stack)
    return x

_drawn_inputs = setup_inputs


def setup_inputs(seed=0):
    import zlib

    import numpy as np

    out = dict(_drawn_inputs(seed))
    spreads = {}
    factors = {'L0_ffn_b_base': 64.0,
     'L0_ffn_W_router': 8.0,
     'L0_ffn_A_stack': 8.0,
     'L0_ffn_B_stack': 8.0}
    for name, (base, spread) in spreads.items():
        noise = np.random.default_rng([zlib.crc32(name.encode()), seed]).standard_normal(out[name].shape)
        drawn = base * np.exp(spread * noise) if base else spread * noise
        out[name] = jnp.asarray(drawn.astype(out[name].dtype))
    for name, factor in factors.items():
        out[name] = (out[name] * factor).astype(out[name].dtype)
    return out
```

```python
from contextlib import ExitStack

import concourse.bass as bass
from concourse import mybir

P = 128
ALU = mybir.AluOpType
ACT = mybir.ActivationFunctionType
F32 = mybir.dt.float32
F32R = mybir.dt.float32r
F16 = mybir.dt.float16
BF16 = mybir.dt.bfloat16
U8 = mybir.dt.uint8
I32 = mybir.dt.int32
U32 = mybir.dt.uint32

CENTRE = 128.0
EPS = 1e-5
RSQRT_SEED = float(0x5F3759DF)
SCALING = 2.0


def xattn_ffn(nc, x, ctx_kv, quant, w_t, bias, ar_t, b_t, out):
    B, S, D = x.shape
    T = B * S // P
    TB = T // B
    K = D // P
    ER = b_t.shape[0]
    EX = 8
    RANK = ER // EX
    AR = ar_t.shape[1] // K
    H = 512
    NH = D // H
    RING = 6
    PAIRS = T // 2
    PPB = TB // 2
    assert ER == P and AR == ER + EX and NH == 2 and D == ctx_kv.shape[1]

    x_tiles = x.rearrange("b (t p) d -> (b t) p d", p=P)
    out_tiles = out.rearrange("b (t p) d -> (b t) p d", p=P)
    ctx_tiles = ctx_kv.rearrange("b (k p) n -> (b k) p n", p=P)
    w_tiles = w_t.rearrange("(k p) n -> k p n", p=P)

    with ExitStack() as stack:
        def sb(name, shape, dt):
            return stack.enter_context(nc.sbuf_tensor(name, shape, dt))

        def sem(name):
            return stack.enter_context(nc.semaphore(name))

        xs = sb("xs", [P, T, D], F32)
        stage = sb("stage", [P, RING, D], F32)
        ctx_u8 = sb("ctx_u8", [P, 3, D], U8)
        a2 = sb("a2", [P, K, D], BF16)
        x_u8 = sb("x_u8", [P, 2, D], U8)
        a1 = sb("a1", [P, 2, D], BF16)
        a1_t = sb("a1_t", [P, 4, K, P], BF16)
        colsum_in = sb("colsum_in", [P, D], F16)
        corr = sb("corr", [P, D], F32)
        bias_sb = sb("bias_sb", [P, D], F32)
        w_hi = sb("w_hi", [P, K, D], F32R)
        w_lo = sb("w_lo", [P, K, D], F32R)
        ar_hi = sb("ar_hi", [P, K, AR], F32R)
        ar_lo = sb("ar_lo", [P, K, AR], F32R)
        b_hi = sb("b_hi", [P, D], F32R)
        b_lo = sb("b_lo", [P, D], F32R)
        y = sb("y", [P, K * AR], F32)
        yt_hi = sb("yt_hi", [P, 2, K, P], F32R)
        yt_lo = sb("yt_lo", [P, 2, K, P], F32R)
        hc = sb("hc", [P, ER], F32)
        hct_hi = sb("hct_hi", [P, P], F32R)
        hct_lo = sb("hct_lo", [P, P], F32R)
        ident = sb("ident", [P, P], F32)
        ident16 = sb("ident16", [P, P], BF16)
        ones16 = sb("ones16", [P, P], F16)
        expert_i = sb("expert_i", [P, ER], I32)
        expert = sb("expert", [P, ER], F32)
        prm = sb("prm", [P, 4], F32)
        inv_s = sb("inv_s", [P, 4], F32)
        con = sb("con", [P, 8], F32)
        bn = sb("bn", [P, 2, 2, 6], F32)
        mv = sb("mv", [P, 2, 2], F32)
        rs = sb("rs", [P, 2, 8], F32)
        q_scale = sb("q_scale", [P, T], F32)
        q_bias = sb("q_bias", [P, T], F32)
        rowsum = sb("rowsum", [P, T], F32)
        row_term = sb("row_term", [P, T], F32)
        y_scale = sb("y_scale", [P, 2], F32)
        y_bias = sb("y_bias", [P, 2], F32)
        wait_pad = sb("wait_pad", [P, 1], F32)
        top = sb("top", [P, 8], F32)
        top_i = sb("top_i", [P, 8], U32)
        top_f = sb("top_f", [P, 8], F32)
        gate = sb("gate", [P, 8], F32)
        c1 = sb("c1", [P, ER], F32)
        c2 = sb("c2", [P, ER], F32)
        cw = sb("cw", [P, ER], F32)
        ps = stack.enter_context(nc.psum_tensor("ps", [P, 8, H], F32))

        s12, d1, d2, col_scale, row_scale, k_d1 = (con[:, i:i + 1] for i in range(6))

        def s1_bank(t):
            return 4 * (t // 2 % 2) + 2 * (t % 2)

        COLSUM_BANK = [(5, 7), (6, 7)]
        OUT_BANK = [0, 4]
        AR_BANK = [2, 3]
        HCT = slice(256, 256 + P)

        def yt_banks(t):
            return slice(2, 4) if t == 0 else slice(6, 8)

        quant_in = sem("quant_in")
        x_in = [sem(f"x_in{t}") for t in range(T)]
        stage_in = [sem(f"stage_in{r}") for r in range(RING)]
        ar_in, b_in, bias_in = sem("ar_in"), sem("b_in"), sem("bias_in")
        stored = sem("stored")
        ident_ready, iota_ready = sem("ident_ready"), sem("iota_ready")
        ident16_ready, ones_ready = sem("ident16_ready"), sem("ones_ready")
        consts_ready = sem("consts_ready")
        vec_step = sem("vec_step")
        q_scaled = sem("q_scaled")
        x_quantised = sem("x_quantised")
        x_centred = sem("x_centred")
        a1_transposed = sem("a1_transposed")
        a1t_ready = sem("a1t_ready")
        ctx_quantised = sem("ctx_quantised")
        ctx_centred = [sem("ctx_centred0"), sem("ctx_centred1")]
        a2_used = sem("a2_used")
        stage1_done = sem("stage1_done")
        summed = sem("summed")
        colsum_added = sem("colsum_added")
        colsum_done = sem("colsum_done")
        corr_ready = sem("corr_ready")
        x1_ready = sem("x1_ready")
        row_ready = sem("row_ready")
        w_hi_ready, w_lo_ready = sem("w_hi_ready"), sem("w_lo_ready")
        ar_hi_ready, ar_lo_ready = sem("ar_hi_ready"), sem("ar_lo_ready")
        b_hi_ready, b_lo_ready = sem("b_hi_ready"), sem("b_lo_ready")
        ln_step = sem("ln_step")
        y_scaled = sem("y_scaled")
        y_ready = sem("y_ready")
        y_transposed = sem("y_transposed")
        yt_hi_ready, yt_lo_ready = sem("yt_hi_ready"), sem("yt_lo_ready")
        main_done = sem("main_done")
        gate_step = sem("gate_step")
        gate_diff = sem("gate_diff")
        gate_exp = sem("gate_exp")
        hc_ready = sem("hc_ready")
        hc_transposed = sem("hc_transposed")
        hct_hi_ready, hct_lo_ready = sem("hct_hi_ready"), sem("hct_lo_ready")
        out_done = sem("out_done")
        bias_added = sem("bias_added")

        def staged(n):
            return stage_in[n % RING], 16 * (n // RING + 1)

        block = stack.enter_context(nc.Block())

        @block.sync
        def _(sp):
            def load_x(t):
                sp.dma_start(xs[:, t, :], x_tiles[t]).then_inc(x_in[t], 16)

            def load_staged(n):
                if n >= RING:
                    m = n - RING
                    if m < B * K:
                        sp.wait_ge(ctx_quantised, m + 1)
                    else:
                        sp.wait_ge(w_hi_ready, m - B * K + 1)
                        sp.wait_ge(w_lo_ready, m - B * K + 1)
                src = ctx_tiles[n] if n < B * K else w_tiles[n - B * K]
                sp.dma_start(stage[:, n % RING, :], src).then_inc(stage_in[n % RING], 16)

            load_x(0)
            sp.dma_start(prm[:, :], quant.partition_broadcast(P)).then_inc(quant_in, 16)
            load_x(1)
            for n in range(4):
                load_staged(n)
            load_x(2)
            load_x(3)
            for n in range(4, K):
                load_staged(n)
            load_x(4)
            load_x(5)
            sp.dma_start(y[:, :], ar_t).then_inc(ar_in, 16)
            load_staged(K)
            load_staged(K + 1)
            load_x(6)
            load_x(7)
            sp.dma_start(bias_sb[:, :], b_t).then_inc(b_in, 16)
            for n in range(K + 2, (B + 1) * K):
                load_staged(n)
            sp.wait_ge(b_hi_ready, 1)
            sp.wait_ge(b_lo_ready, 1)
            sp.dma_start(bias_sb[:, :], bias.partition_broadcast(P)).then_inc(bias_in, 16)
            with sp.Fori(0, T - 1) as t:
                sp.wait_ge(summed, T + t + 1)
                sp.dma_start(out_tiles[t], xs[:, t, :]).then_inc(stored, 16)
            for h in range(NH):
                sp.wait_ge(summed, 2 * T + h)
                sp.dma_start(out_tiles[T - 1][:, h * H:(h + 1) * H],
                             xs[:, T - 1, h * H:(h + 1) * H]).then_inc(stored, 16)
            sp.wait_ge(stored, 16 * (T + 1))

        @block.gpsimd
        def _(pool):
            nc.gpsimd.memset(ident[:, :], 0.0).then_inc(ident_ready, 1)
            pool.wait_ge(ident_ready, 1)
            nc.gpsimd.affine_select(out=ident[:, :], in_=ident[:, :], compare_op=ALU.not_equal, fill=1.0,
                                    base=0, pattern=[[-1, P]], channel_multiplier=1).then_inc(ident_ready, 1)
            nc.gpsimd.iota(expert_i[:, :], pattern=[[1, EX], [0, RANK]], base=0,
                           channel_multiplier=0).then_inc(iota_ready, 1)

            def add_colsum(b, k):
                pool.wait_ge(ctx_centred[b], k + 1)
                if k == 1:
                    if b:
                        pool.wait_ge(colsum_done, b)
                    nc.gpsimd.tensor_tensor(colsum_in[:, :], a2[:, 0, :], a2[:, 1, :],
                                            ALU.add).then_inc(colsum_added, 1)
                else:
                    pool.wait_ge(colsum_added, b * (K - 1) + k - 1)
                    nc.gpsimd.tensor_tensor(colsum_in[:, :], colsum_in[:, :], a2[:, k, :],
                                            ALU.add).then_inc(colsum_added, 1)

            def add_corr(t):
                pool.wait_ge(summed, t + 1)
                pool.wait_ge(corr_ready, t // TB + 1)
                nc.gpsimd.tensor_tensor(xs[:, t, :], xs[:, t, :], corr[:, :], ALU.add).then_inc(x1_ready, 1)

            def centre_ctx(k):
                n = K + k
                pool.wait_ge(ctx_quantised, n + 1)
                pool.wait_ge(a2_used, k + 1)
                nc.gpsimd.tensor_scalar(a2[:, k, :], ctx_u8[:, n % 3, :], -CENTRE, 1.0,
                                        ALU.add, ALU.mult).then_inc(ctx_centred[1], 1)

            def add_bias(t):
                pool.wait_ge(y_ready, t + 1)
                nc.gpsimd.tensor_tensor(xs[:, t, :], xs[:, t, :], bias_sb[:, :],
                                        ALU.add).then_inc(bias_added, 1)

            for k in range(1, K):
                add_colsum(0, k)
            centre_ctx(0)
            centre_ctx(1)
            for t in range(TB):
                add_corr(t)
                if 2 * t + 3 < K:
                    centre_ctx(2 * t + 2)
                    centre_ctx(2 * t + 3)
            for k in range(1, K):
                add_colsum(1, k)
            pool.wait_ge(bias_in, 16)
            add_bias(0)
            for t in range(TB, T):
                add_corr(t)
            with pool.Fori(1, T) as t:
                add_bias(t)

        @block.scalar
        def _(act):
            def quantise_x(t):
                act.wait_ge(x_in[t], 16)
                act.wait_ge(q_scaled, t + 1)
                if t >= 2:
                    act.wait_ge(x_centred, t - 1)
                nc.scalar.activation(x_u8[:, t % 2, :], xs[:, t, :], ACT.Identity, bias=q_bias[:, t:t + 1],
                                     scale=q_scale[:, t:t + 1]).then_inc(x_quantised, 1)

            def centre_x(t):
                act.wait_ge(x_quantised, t + 1)
                if t >= 2:
                    act.wait_ge(a1_transposed, t - 1)
                nc.scalar.activation(a1[:, t % 2, :], x_u8[:, t % 2, :], ACT.Copy, bias=-CENTRE,
                                     accum_out=rowsum[:, t:t + 1]).then_inc(x_centred, 1)

            def quantise_ctx(n):
                act.wait_ge(*staged(n))
                if n >= 3:
                    m = n - 3
                    act.wait_ge(ctx_centred[m // K], m % K + 1)
                nc.scalar.activation(ctx_u8[:, n % 3, :], stage[:, n % RING, :], ACT.Identity,
                                     bias=prm[:, 3:4], scale=inv_s[:, 2:3]).then_inc(ctx_quantised, 1)

            def make_corr(b):
                act.wait_ge(colsum_done, b + 1)
                if b:
                    act.wait_ge(x1_ready, b * TB)
                lo, hi = COLSUM_BANK[b]
                nc.scalar.activation(corr[:, :].rearrange("p (h n) -> p h n", h=NH),
                                     ps[:, lo:hi + 1:hi - lo, :], ACT.Identity,
                                     scale=col_scale).then_inc(corr_ready, 1)

            def split_w(k):
                act.wait_ge(*staged(B * K + k))
                nc.scalar.activation(w_hi[:, k, :], stage[:, (B * K + k) % RING, :],
                                     ACT.Copy).then_inc(w_hi_ready, 1)

            def make_y(t, par):
                act.wait_ge(y_scaled, t + 1)
                act.wait_ge(y_transposed, t) if par is not None else act.wait_ge(ar_lo_ready, 1)
                p = par or 0
                nc.scalar.activation(y[:, 0:D], xs[:, t, :], ACT.Identity, bias=y_bias[:, p:p + 1],
                                     scale=y_scale[:, p:p + 1]).then_inc(y_ready, 1)

            def split_yt(t, p, banks):
                act.wait_ge(y_transposed, t + 1)
                nc.scalar.activation(yt_hi[:, p, :, :].rearrange("p (h k) c -> p h (k c)", h=2),
                                     ps[:, banks, :], ACT.Copy).then_inc(yt_hi_ready, 1)

            def gate_weight(t):
                act.wait_ge(gate_diff, t + 1)
                nc.scalar.activation(gate[:, 1:2], gate[:, 0:1], ACT.Exp).then_inc(gate_exp, 1)

            def split_hct(t, p):
                act.wait_ge(hc_transposed, t + 1)
                nc.scalar.activation(hct_hi[:, :], ps[:, AR_BANK[p], HCT], ACT.Copy).then_inc(hct_hi_ready, 1)

            act.wait_ge(consts_ready, 1)
            act.wait_ge(quant_in, 16)
            for t in (0, 1):
                quantise_x(t)
                centre_x(t)
            for n in range(4):
                quantise_ctx(n)
            for t in (2, 3):
                quantise_x(t)
                centre_x(t)
            for n in range(4, K):
                quantise_ctx(n)
            for t in (4, 5):
                quantise_x(t)
                centre_x(t)
            quantise_ctx(K)
            quantise_ctx(K + 1)
            make_corr(0)
            act.wait_ge(ar_in, 16)
            nc.scalar.activation(ar_hi[:, :, :].rearrange("p k c -> p (k c)"), y[:, :],
                                 ACT.Copy).then_inc(ar_hi_ready, 1)
            for n in range(K + 2, K + 4):
                quantise_ctx(n)
            for t in (6, 7):
                quantise_x(t)
                centre_x(t)
            for n in range(K + 4, B * K):
                quantise_ctx(n)
            act.wait_ge(b_in, 16)
            nc.scalar.activation(b_hi[:, :], bias_sb[:, :], ACT.Copy).then_inc(b_hi_ready, 1)
            make_y(0, None)
            split_w(0)
            split_w(1)
            split_yt(0, 0, yt_banks(0))
            for k in range(2, K):
                split_w(k)
            make_y(1, 1)
            split_yt(1, 1, yt_banks(1))
            make_corr(1)

            def tile(t, p):
                make_y(t + 1, 1 - p)
                gate_weight(t - 1)
                split_hct(t - 1, 1 - p)
                split_yt(t + 1, 1 - p, yt_banks(1))

            with act.Fori(0, (T - 2) // 2) as i:
                tile(2 * i + 1, 1)
                tile(2 * i + 2, 0)
            for t in (T - 2, T - 1):
                gate_weight(t)
                split_hct(t, t % 2)

        @block.vector
        def _(dve):
            steps = [0]

            def then(ins):
                steps[0] += 1
                ins.then_inc(vec_step, 1)
                dve.wait_ge(vec_step, steps[0])

            def rsqrt_steps(var, r, tmp, link):
                half, shifted, t = tmp[:, 0:1], tmp[:, 1:2], tmp[:, 2:3]
                nc.vector.tensor_scalar(half, var, EPS, -0.5, ALU.add, ALU.mult)
                link(nc.vector.tensor_scalar(shifted, var, EPS, None, ALU.add))
                link(nc.vector.tensor_scalar(shifted.bitcast(I32), shifted.bitcast(I32), 1, None,
                                             ALU.logical_shift_right))
                link(nc.vector.tensor_scalar(r.bitcast(I32), shifted.bitcast(I32), -1.0, RSQRT_SEED,
                                             ALU.mult, ALU.add))
                for _ in range(3):
                    link(nc.vector.scalar_tensor_tensor(out=t, in0=r, scalar=half, in1=r,
                                                        op0=ALU.mult, op1=ALU.mult))
                    link(nc.vector.scalar_tensor_tensor(out=r, in0=t, scalar=1.5, in1=r,
                                                        op0=ALU.add, op1=ALU.mult))

            LN_LINKS = 11

            def layernorm_steps(t, p, link):
                link2 = nc.vector.bn_stats(bn[:, p, 0, :], xs[:, t, 0:H])
                link(nc.vector.bn_stats(bn[:, p, 1, :], xs[:, t, H:D]))
                del link2
                nc.vector.memset(wait_pad[:, :], 0.0)
                link(nc.vector.bn_aggr(mv[:, p, :], bn[:, p, :, :].rearrange("p a b -> p (a b)")))
                rsqrt_steps(mv[:, p, 1:2], rs[:, p, 4:5], rs[:, p, :], link)

            def scale_x(t):
                p = t % 2
                dve.wait_ge(x_in[t], 16)
                layernorm_steps(t, p, then)
                then(nc.vector.tensor_scalar(q_scale[:, t:t + 1], rs[:, p, 4:5], inv_s[:, 0:1], None, ALU.mult))
                then(nc.vector.scalar_tensor_tensor(out=rs[:, p, 5:6], in0=mv[:, p, 0:1], scalar=-1.0,
                                                    in1=q_scale[:, t:t + 1], op0=ALU.mult, op1=ALU.mult))
                nc.vector.tensor_scalar(q_bias[:, t:t + 1], rs[:, p, 5:6], prm[:, 1:2], None,
                                        ALU.add).then_inc(q_scaled, 1)

            def take_a1t(t):
                dve.wait_ge(a1_transposed, t + 1)
                if t >= 4:
                    dve.wait_ge(stage1_done, t - 3)
                nc.vector.tensor_copy(a1_t[:, t % 4, :, :].rearrange("p k c -> p (k c)"),
                                      ps[:, s1_bank(t), :].bitcast(BF16)).then_inc(a1t_ready, 1)

            def centre_ctx(k):
                dve.wait_ge(ctx_quantised, k + 1)
                nc.vector.tensor_scalar(a2[:, k, :], ctx_u8[:, k % 3, :], -CENTRE, None,
                                        ALU.add).then_inc(ctx_centred[0], 1)

            def sum_x1(t):
                dve.wait_ge(stage1_done, t + 1)
                dve.wait_ge(x_quantised, t + 1)
                nc.vector.scalar_tensor_tensor(
                    out=xs[:, t, :].rearrange("p (h n) -> p h n", h=NH),
                    in0=ps[:, s1_bank(t):s1_bank(t) + 2, :], scalar=s12,
                    in1=xs[:, t, :].rearrange("p (h n) -> p h n", h=NH),
                    op0=ALU.mult, op1=ALU.add).then_inc(summed, 1)

            def make_row_term(t):
                dve.wait_ge(x_centred, t + 1)
                nc.vector.tensor_scalar(row_term[:, t:t + 1], rowsum[:, t:t + 1], k_d1, row_scale,
                                        ALU.add, ALU.mult).then_inc(row_ready, 1)

            def ln_link(t):
                n = [0]

                def link(ins):
                    n[0] += 1
                    ins.then_inc(ln_step, 1)
                    dve.wait_ge(ln_step, t * (LN_LINKS + 1) + n[0])
                return link

            def scale_y(t, p, first=False):
                dve.wait_ge(x1_ready, t + 1)
                if not first:
                    dve.wait_ge(y_ready, t - 1)
                link = ln_link(t)
                layernorm_steps(t, p, link)
                link(nc.vector.tensor_copy(y_scale[:, p:p + 1], rs[:, p, 4:5]))
                nc.vector.scalar_tensor_tensor(out=y_bias[:, p:p + 1], in0=mv[:, p, 0:1], scalar=-1.0,
                                               in1=rs[:, p, 4:5], op0=ALU.mult,
                                               op1=ALU.mult).then_inc(y_scaled, 1)

            def split_w(k):
                dve.wait_ge(w_hi_ready, k + 1)
                nc.vector.tensor_tensor(w_lo[:, k, :], stage[:, (B * K + k) % RING, :],
                                        w_hi[:, k, :].bitcast(F32), ALU.subtract).then_inc(w_lo_ready, 1)

            def split_yt(t, p, banks):
                dve.wait_ge(yt_hi_ready, t + 1)
                nc.vector.tensor_tensor(yt_lo[:, p, :, :].rearrange("p (h k) c -> p h (k c)", h=2),
                                        ps[:, banks, :],
                                        yt_hi[:, p, :, :].bitcast(F32).rearrange("p (h k) c -> p h (k c)", h=2),
                                        ALU.subtract).then_inc(yt_lo_ready, 1)

            GATE_LINKS = 8

            def gate_tile(t, p):
                n = [0]

                def link(ins):
                    n[0] += 1
                    ins.then_inc(gate_step, 1)
                    dve.wait_ge(gate_step, t * GATE_LINKS + n[0])

                logits = ps[:, AR_BANK[p], ER:AR]
                dve.wait_ge(main_done, t + 1)
                nc.vector.memset(wait_pad[:, :], 0.0)
                link(nc.vector.max(top[:, :], logits))
                nc.vector.tensor_tensor(gate[:, 0:1], top[:, 1:2], top[:, 0:1], ALU.subtract).then_inc(gate_diff, 1)
                link(nc.vector.max_index(top_i[:, :], top[:, :], logits))
                link(nc.vector.tensor_copy(top_f[:, :], top_i[:, :]))
                dve.wait_ge(gate_exp, t + 1)
                link(nc.vector.tensor_scalar(gate[:, 2:3], gate[:, 1:2], 1.0, 1.0 / SCALING, ALU.add, ALU.mult))
                link(nc.vector.reciprocal(gate[:, 3:4], gate[:, 2:3]))
                link(nc.vector.tensor_scalar(gate[:, 4:5], gate[:, 1:2], gate[:, 3:4], None, ALU.mult))
                nc.vector.tensor_scalar(c1[:, :], expert[:, :], top_f[:, 0:1], gate[:, 3:4],
                                        ALU.is_equal, ALU.mult)
                link(nc.vector.tensor_scalar(c2[:, :], expert[:, :], top_f[:, 1:2], gate[:, 4:5],
                                             ALU.is_equal, ALU.mult))
                link(nc.vector.tensor_tensor(cw[:, :], c1[:, :], c2[:, :], ALU.add))
                nc.vector.tensor_tensor(hc[:, :], ps[:, AR_BANK[p], 0:ER], cw[:, :],
                                        ALU.mult).then_inc(hc_ready, 1)

            def split_hct(t, p):
                dve.wait_ge(hct_hi_ready, t + 1)
                nc.vector.tensor_tensor(hct_lo[:, :], ps[:, AR_BANK[p], HCT], hct_hi[:, :].bitcast(F32),
                                        ALU.subtract).then_inc(hct_lo_ready, 1)

            def sum_out(t, p, h0, h1):
                nc.vector.scalar_tensor_tensor(
                    out=xs[:, t, h0 * H:h1 * H].rearrange("p (h n) -> p h n", n=H),
                    in0=ps[:, OUT_BANK[p] + h0:OUT_BANK[p] + h1, :],
                    scalar=row_term[:, bass.ds(t, 1)],
                    in1=xs[:, t, h0 * H:h1 * H].rearrange("p (h n) -> p h n", n=H),
                    op0=ALU.add, op1=ALU.add).then_inc(summed, 1)

            nc.vector.memset(ones16[:, :], 1.0).then_inc(ones_ready, 1)
            dve.wait_ge(quant_in, 16)
            nc.vector.reciprocal(inv_s[:, 0:1], prm[:, 0:1])
            then(nc.vector.reciprocal(inv_s[:, 2:3], prm[:, 2:3]))
            nc.vector.tensor_tensor(s12, prm[:, 0:1], prm[:, 2:3], ALU.mult)
            nc.vector.tensor_scalar(d1, prm[:, 1:2], -1.0, CENTRE, ALU.mult, ALU.add)
            then(nc.vector.tensor_scalar(d2, prm[:, 3:4], -1.0, CENTRE, ALU.mult, ALU.add))
            nc.vector.tensor_tensor(col_scale, d1, s12, ALU.mult)
            nc.vector.tensor_tensor(row_scale, d2, s12, ALU.mult)
            nc.vector.tensor_scalar(k_d1, d1, float(D), None, ALU.mult).then_inc(consts_ready, 1)
            dve.wait_ge(consts_ready, 1)
            scale_x(0)
            dve.wait_ge(ident_ready, 2)
            nc.vector.tensor_copy(ident16[:, :], ident[:, :]).then_inc(ident16_ready, 1)
            scale_x(1)
            dve.wait_ge(iota_ready, 1)
            then(nc.vector.tensor_copy(expert[:, :], expert_i[:, :]))
            take_a1t(0)
            take_a1t(1)
            for k in range(4):
                centre_ctx(k)
            scale_x(2)
            scale_x(3)
            for k in range(4, K):
                centre_ctx(k)
                if k == 5:
                    take_a1t(2)
                if k == 7:
                    take_a1t(3)
            sum_x1(0)
            sum_x1(1)
            scale_x(4)
            scale_x(5)
            take_a1t(4)
            take_a1t(5)
            sum_x1(2)
            sum_x1(3)
            scale_x(6)
            scale_x(7)
            dve.wait_ge(ar_hi_ready, 1)
            nc.vector.tensor_tensor(ar_lo[:, :, :].rearrange("p k c -> p (k c)"), y[:, :],
                                    ar_hi[:, :, :].bitcast(F32).rearrange("p k c -> p (k c)"),
                                    ALU.subtract).then_inc(ar_lo_ready, 1)
            scale_y(0, 0, first=True)
            take_a1t(6)
            take_a1t(7)
            dve.wait_ge(b_hi_ready, 1)
            nc.vector.tensor_tensor(b_lo[:, :], bias_sb[:, :], b_hi[:, :].bitcast(F32),
                                    ALU.subtract).then_inc(b_lo_ready, 1)
            sum_x1(4)
            sum_x1(5)
            split_yt(0, 0, yt_banks(0))
            split_w(0)
            split_w(1)
            scale_y(1, 1, first=True)
            for k in range(2, K):
                split_w(k)
                if k == 4:
                    sum_x1(6)
                if k == 5:
                    sum_x1(7)
            for t in range(T):
                make_row_term(t)
            dve.wait_ge(row_ready, T)
            split_yt(1, 1, yt_banks(1))

            def tile(t, p):
                scale_y(t + 1, 1 - p)
                gate_tile(t - 1, 1 - p)
                split_hct(t - 1, 1 - p)
                split_yt(t + 1, 1 - p, yt_banks(1))
                dve.wait_ge(out_done, t)
                dve.wait_ge(bias_added, t)
                sum_out(t - 1, 1 - p, 0, NH)

            with dve.Fori(0, (T - 2) // 2) as i:
                tile(2 * i + 1, 1)
                tile(2 * i + 2, 0)
            gate_tile(T - 2, 0)
            split_hct(T - 2, 0)
            dve.wait_ge(out_done, T - 1)
            dve.wait_ge(bias_added, T - 1)
            sum_out(T - 2, 0, 0, NH)
            gate_tile(T - 1, 1)
            split_hct(T - 1, 1)
            dve.wait_ge(bias_added, T)
            for h in range(NH):
                dve.wait_ge(out_done, T + h)
                sum_out(T - 1, 1, h, h + 1)

        @block.tensor
        def _(pe):
            def transpose_a1(t):
                pe.wait_ge(x_centred, t + 1)
                if t >= 4:
                    pe.wait_ge(summed, t - 3)
                bank = ps[:, s1_bank(t), :].bitcast(BF16)
                for k in range(K):
                    last = nc.tensor.transpose(bank[:, k * P:(k + 1) * P], a1[:, t % 2, k * P:(k + 1) * P],
                                               ident16[:, :])
                last.then_inc(a1_transposed, 1)

            def stage1(q, between):
                b = q // PPB
                pe.wait_ge(a1t_ready, 2 * q + 2)
                if q >= 2:
                    pe.wait_ge(summed, 2 * q - 2)
                for k in range(K):
                    pe.wait_ge(ctx_centred[b], k + 1)
                    for t in (2 * q, 2 * q + 1):
                        for h in range(NH):
                            last = nc.tensor.matmul(ps[:, s1_bank(t) + h, :], a1_t[:, t % 4, k, :],
                                                    a2[:, k, h * H:(h + 1) * H],
                                                    start=(k == 0), stop=(k == K - 1))
                        if k == K - 1:
                            last.then_inc(stage1_done, 1)
                    if q % PPB == PPB - 1 and k < K - 1:
                        last.then_inc(a2_used, 1)
                    if k in between:
                        between[k]()
                if q % PPB == PPB - 1:
                    nc.tensor.ldweights(ident16[:, :]).then_inc(a2_used, 1)

            def colsum(b):
                pe.wait_ge(colsum_added, (b + 1) * (K - 1))
                for h in range(NH):
                    last = nc.tensor.matmul(ps[:, COLSUM_BANK[b][h], :], ones16[:, :],
                                            colsum_in[:, h * H:(h + 1) * H], start=True, stop=True)
                last.then_inc(colsum_done, 1)

            def transpose_y(t, banks):
                pe.wait_ge(y_ready, t + 1)
                for k in range(K):
                    last = nc.tensor.transpose(ps[:, banks.start + k // 4, (k % 4) * P:(k % 4 + 1) * P],
                                               y[:, k * P:(k + 1) * P], ident[:, :])
                last.then_inc(y_transposed, 1)

            def transpose_hc(t, p):
                pe.wait_ge(hc_ready, t + 1)
                nc.tensor.transpose(ps[:, AR_BANK[p], HCT], hc[:, :], ident[:, :]).then_inc(hc_transposed, 1)

            def lora(t, p, incs):
                pe.wait_ge(hct_lo_ready, t + 1)
                for h in range(NH):
                    dst = ps[:, OUT_BANK[p] + h, :]
                    cols = slice(h * H, (h + 1) * H)
                    nc.tensor.matmul(dst, hct_hi[:, :], b_hi[:, cols], start=False, stop=False)
                    nc.tensor.matmul(dst, hct_hi[:, :], b_lo[:, cols], start=False, stop=False)
                    last = nc.tensor.matmul(dst, hct_lo[:, :], b_hi[:, cols], start=False, stop=True)
                    if h in incs:
                        last.then_inc(out_done, 1)

            def main(t, p, between, first=False):
                out_ps, ar_ps = OUT_BANK[p], ps[:, AR_BANK[p], 0:AR]
                pe.wait_ge(yt_lo_ready, t + 1)
                if first:
                    pe.wait_ge(ar_lo_ready, 1)
                for k in range(K):
                    if first:
                        pe.wait_ge(w_lo_ready, k + 1)
                    hi, lo = yt_hi[:, p, k, :], yt_lo[:, p, k, :]
                    start, stop = k == 0, k == K - 1
                    for h in range(NH):
                        cols = slice(h * H, (h + 1) * H)
                        nc.tensor.matmul(ps[:, out_ps + h, :], hi, w_hi[:, k, cols], start=start, stop=False)
                        nc.tensor.matmul(ps[:, out_ps + h, :], hi, w_lo[:, k, cols], start=False, stop=False)
                    nc.tensor.matmul(ar_ps, hi, ar_hi[:, k, :], start=start, stop=False)
                    nc.tensor.matmul(ar_ps, hi, ar_lo[:, k, :], start=False, stop=False)
                    last = nc.tensor.matmul(ar_ps, lo, ar_hi[:, k, :], start=False, stop=stop)
                    if stop:
                        last.then_inc(main_done, 1)
                    for h in range(NH):
                        cols = slice(h * H, (h + 1) * H)
                        nc.tensor.matmul(ps[:, out_ps + h, :], lo, w_hi[:, k, cols], start=False, stop=False)
                    if k in between:
                        between[k]()

            pe.wait_ge(ident16_ready, 1)
            transpose_a1(0)
            transpose_a1(1)
            stage1(0, {3: lambda: transpose_a1(2), 5: lambda: transpose_a1(3)})
            stage1(1, {5: lambda: transpose_a1(4), 6: lambda: transpose_a1(5)})
            pe.wait_ge(ones_ready, 1)
            pe.wait_ge(summed, TB)
            colsum(0)
            stage1(2, {4: lambda: transpose_a1(6), 6: lambda: transpose_a1(7)})
            pe.wait_ge(corr_ready, 1)
            pe.wait_ge(ident_ready, 2)

            def first_y():
                pe.wait_ge(summed, TB + 2)
                transpose_y(0, yt_banks(0))
            stage1(3, {6: first_y})

            def second_y():
                pe.wait_ge(summed, T)
                transpose_y(1, yt_banks(1))

            def second_colsum():
                pe.wait_ge(yt_hi_ready, 2)
                pe.wait_ge(yt_lo_ready, 2)
                colsum(1)
            main(0, 0, {4: second_y, 7: second_colsum}, first=True)
            pe.wait_ge(b_lo_ready, 1)

            def tile(t, p):
                def next_y():
                    pe.wait_ge(corr_ready, 2)
                    transpose_y(t + 1, yt_banks(1))
                pe.wait_ge(summed, T + t - 1)
                main(t, p, {2: lambda: transpose_hc(t - 1, 1 - p), 3: next_y,
                            5: lambda: lora(t - 1, 1 - p, (NH - 1,))})

            with pe.Fori(0, (T - 2) // 2) as i:
                tile(2 * i + 1, 1)
                tile(2 * i + 2, 0)
            last = T - 1
            pe.wait_ge(summed, T + last - 1)
            main(last, 1, {2: lambda: transpose_hc(last - 1, 0), 5: lambda: lora(last - 1, 0, (NH - 1,))})
            transpose_hc(last, 1)
            lora(last, 1, range(NH))


def kernel(x, ctx_4096, L0_xattn_x1_scale, L0_xattn_x1_zp, L0_xattn_x2_scale, L0_xattn_x2_zp,
           L0_ffn_W_base, L0_ffn_b_base, L0_ffn_W_router, L0_ffn_A_stack, L0_ffn_B_stack):
    import numpy as np
    import concourse.bacc as bacc
    from concourse.bass_utils import run_bass_kernel_spmd as run

    D = x.shape[-1]
    experts, rank, _ = L0_ffn_A_stack.shape
    ar = np.concatenate([np.reshape(L0_ffn_A_stack, (experts * rank, D)), np.asarray(L0_ffn_W_router)])
    ar = np.transpose(np.reshape(ar.T, (D // P, P, experts * rank + experts)), (1, 0, 2))
    arrays = {
        "x": x, "ctx_kv": ctx_4096,
        "quant": np.concatenate([np.reshape(v, (1,)) for v in (L0_xattn_x1_scale, L0_xattn_x1_zp,
                                                               L0_xattn_x2_scale, L0_xattn_x2_zp)]),
        "w_t": np.transpose(L0_ffn_W_base), "bias": L0_ffn_b_base,
        "ar_t": np.reshape(ar, (P, -1)),
        "b_t": np.reshape(np.transpose(L0_ffn_B_stack, (0, 2, 1)), (experts * rank, D)),
    }
    arrays = {name: np.ascontiguousarray(a) for name, a in arrays.items()}
    nc = bacc.Bacc("TRN2", target_bir_lowering=False, num_devices=1)
    args = {name: nc.dram_tensor(f"in_{name}", a.shape, mybir.dt.from_np(a.dtype), kind="ExternalInput").ap()
            for name, a in arrays.items()}
    args["out"] = nc.dram_tensor("out_dram", x.shape, F32, kind="ExternalOutput").ap()
    xattn_ffn(nc, **args)
    result = run(nc, [{f"in_{name}": a for name, a in arrays.items()}], core_ids=[0])
    return result.results[0]["out_dram"]
```

```python
from contextlib import ExitStack

import concourse.bass as bass
from concourse import mybir

P = 128
ALU = mybir.AluOpType
ACT = mybir.ActivationFunctionType
F32 = mybir.dt.float32
F32R = mybir.dt.float32r
F16 = mybir.dt.float16
BF16 = mybir.dt.bfloat16
U8 = mybir.dt.uint8
I32 = mybir.dt.int32
U32 = mybir.dt.uint32

CENTRE = 128.0
EPS = 1e-5
Y_SCALE = 1024.0
AR_FLOOR = 1e-30
EXPONENT = 0x7F800000
RSQRT_SEED = float(0x5F3759DF)
SCALING = 2.0


def xattn_ffn(nc, x, ctx_kv, quant, w_t, bias, ar_t, b_t, out):
    B, S, D = x.shape
    T = B * S // P
    TB = T // B
    K = D // P
    ER = b_t.shape[0]
    EX = 8
    RANK = ER // EX
    AR = ar_t.shape[1] // K
    H = 512
    NH = D // H
    WARM_UP = 30
    RING = 6
    PAIRS = T // 2
    PPB = TB // 2
    assert ER == P and AR == ER + EX and NH == 2 and D == ctx_kv.shape[1]

    x_tiles = x.rearrange("b (t p) d -> (b t) p d", p=P)
    out_tiles = out.rearrange("b (t p) d -> (b t) p d", p=P)
    ctx_tiles = ctx_kv.rearrange("b (k p) n -> (b k) p n", p=P)
    w_tiles = w_t.rearrange("(k p) n -> k p n", p=P)

    with ExitStack() as stack:
        def sb(name, shape, dt):
            return stack.enter_context(nc.sbuf_tensor(name, shape, dt))

        def sem(name):
            return stack.enter_context(nc.semaphore(name))

        xs = sb("xs", [P, T, D], F32)
        stage = sb("stage", [P, RING, D], F32)
        ctx_u8 = sb("ctx_u8", [P, 3, D], U8)
        a2 = sb("a2", [P, K, D], BF16)
        x_u8 = sb("x_u8", [P, 2, D], U8)
        a1 = sb("a1", [P, 2, D], BF16)
        a1_t = sb("a1_t", [P, 4, K, P], BF16)
        corr = sb("corr", [P, B, D], F32)
        bias_sb = sb("bias_sb", [P, D], F32)
        w_hi = sb("w_hi", [P, K, D], F32R)
        w_lo = sb("w_lo", [P, K, D], F32R)
        ar_hi = sb("ar_hi", [P, K, AR], F16)
        ar_lo = sb("ar_lo", [P, K, AR], F16)
        b_hi = sb("b_hi", [P, D], F32R)
        b_lo = sb("b_lo", [P, D], F32R)
        y = sb("y", [P, K * AR], F32)
        yt_hi = sb("yt_hi", [P, 2, K, P], F32R)
        yt_lo = sb("yt_lo", [P, 2, K, P], F32R)
        yt_hi16 = sb("yt_hi16", [P, K, P], F16)
        yt_lo16 = sb("yt_lo16", [P, K, P], F16)
        hc = sb("hc", [P, ER], F32)
        hct_hi = sb("hct_hi", [P, P], F32R)
        hct_lo = sb("hct_lo", [P, P], F32R)
        ident = sb("ident", [P, P], F32)
        ident16 = sb("ident16", [P, P], BF16)
        ones16 = sb("ones16", [P, 3 * P], BF16)
        expert_i = sb("expert_i", [P, ER], I32)
        expert = sb("expert", [P, ER], F32)
        prm = sb("prm", [P, 4], F32)
        inv_s = sb("inv_s", [P, 4], F32)
        con = sb("con", [P, 8], F32)
        bn = sb("bn", [P, 2, 2, 6], F32)
        mv = sb("mv", [P, 2, 2], F32)
        rsq = sb("rsq", [P, 6, 2], F32)
        peak = sb("peak", [P, 2], F32)
        peak_all = sb("peak_all", [P, 2], F32)
        ar_scale = sb("ar_scale", [P, 2], F32)
        ar_undo = sb("ar_undo", [P, 2], F32)
        q_scale = sb("q_scale", [P, T], F32)
        q_bias = sb("q_bias", [P, T], F32)
        rowsum = sb("rowsum", [P, T], F32)
        row_term = sb("row_term", [P, T], F32)
        y_scale = sb("y_scale", [P, 2], F32)
        y_bias = sb("y_bias", [P, 2], F32)
        wait_pad = sb("wait_pad", [P, 1], F32)
        top = sb("top", [P, 8], F32)
        top_i = sb("top_i", [P, 8], U32)
        top_f = sb("top_f", [P, 8], F32)
        gate = sb("gate", [P, 8], F32)
        c1 = sb("c1", [P, ER], F32)
        c2 = sb("c2", [P, ER], F32)
        cw = sb("cw", [P, ER], F32)
        ps = stack.enter_context(nc.psum_tensor("ps", [P, 8, H], F32))

        s12, d1, d2, col_scale, row_scale, k_d1, den_scale = (con[:, i:i + 1] for i in range(7))

        def s1_bank(t):
            return 4 * (t // 2 % 2) + 2 * (t % 2)

        def a1_bank(t):
            return 4 * (t // 2 % 2) + t % 2

        COLSUM_BANKS = slice(6, 8)
        OUT_BANK = [0, 4]
        AR_BANK = 2
        HCT = slice(256, 256 + P)

        def yt_banks(t):
            return slice(0, 2) if t == 0 else slice(6, 8)

        quant_in = sem("quant_in")
        x_in = [sem(f"x_in{t}") for t in range(T)]
        stage_in = [sem(f"stage_in{r}") for r in range(RING)]
        ar_in, b_in, bias_in = sem("ar_in"), sem("b_in"), sem("bias_in")
        stored = sem("stored")
        ident_ready, iota_ready = sem("ident_ready"), sem("iota_ready")
        ident16_ready, ones_ready = sem("ident16_ready"), sem("ones_ready")
        consts_ready = sem("consts_ready")
        vec_step = sem("vec_step")
        x_statistics = sem("x_statistics")
        q_scaled = sem("q_scaled")
        x_quantised = sem("x_quantised")
        x_centred = sem("x_centred")
        a1_transposed = sem("a1_transposed")
        a1t_ready = sem("a1t_ready")
        ctx_quantised = sem("ctx_quantised")
        ctx_centred = sem("ctx_centred")
        a2_used = sem("a2_used")
        stage1_done = sem("stage1_done")
        summed = sem("summed")
        colsum_done = sem("colsum_done")
        corr_ready = sem("corr_ready")
        x1_ready = sem("x1_ready")
        row_ready = sem("row_ready")
        w_hi_ready = sem("w_hi_ready")
        w_lo_ready = [sem(f"w_lo_ready{k}") for k in range(K)]
        peak_ready, peak_all_ready, ar_scaled = sem("peak_ready"), sem("peak_all_ready"), sem("ar_scaled")
        ar_hi_ready, ar_lo_ready = sem("ar_hi_ready"), sem("ar_lo_ready")
        b_hi_ready, b_lo_ready = sem("b_hi_ready"), sem("b_lo_ready")
        ln_step = sem("ln_step")
        y_scaled = sem("y_scaled")
        y_ready = sem("y_ready")
        y_transposed = sem("y_transposed")
        yt_hi_ready, yt_lo_ready = sem("yt_hi_ready"), sem("yt_lo_ready")
        yt_hi16_ready, yt_lo16_ready = sem("yt_hi16_ready"), sem("yt_lo16_ready")
        ar_done = sem("ar_done")
        gate_step = sem("gate_step")
        gate_diff = sem("gate_diff")
        gate_exp = sem("gate_exp")
        hc_ready = sem("hc_ready")
        hc_transposed = sem("hc_transposed")
        hct_hi_ready, hct_lo_ready = sem("hct_hi_ready"), sem("hct_lo_ready")
        out_done = sem("out_done")
        bias_added = sem("bias_added")

        def staged(n):
            return stage_in[n % RING], 16 * (n // RING + 1)

        block = stack.enter_context(nc.Block())

        @block.sync
        def _(sp):
            def load_x(t):
                sp.dma_start(xs[:, t, :], x_tiles[t]).then_inc(x_in[t], 16)

            def load_staged(n):
                if n >= RING:
                    m = n - RING
                    if m < B * K:
                        sp.wait_ge(ctx_quantised, m + 1)
                    else:
                        sp.wait_ge(w_hi_ready, m - B * K + 1)
                        sp.wait_ge(w_lo_ready[m - B * K], 1)
                src = ctx_tiles[n] if n < B * K else w_tiles[n - B * K]
                sp.dma_start(stage[:, n % RING, :], src).then_inc(stage_in[n % RING], 16)

            sp.dma_start(prm[:, :], quant.partition_broadcast(P)).then_inc(quant_in, 16)
            load_x(0)
            load_x(1)
            load_staged(0)
            load_staged(1)
            load_x(2)
            load_x(3)
            for n in range(2, K - 1):
                load_staged(n)
            sp.dma_start(y[:, :], ar_t).then_inc(ar_in, 16)
            load_staged(K - 1)
            load_x(4)
            load_x(5)
            load_staged(K)
            load_staged(K + 1)
            load_x(6)
            load_x(7)
            for n in range(K + 2, B * K + 2):
                load_staged(n)
            sp.dma_start(bias_sb[:, :], b_t).then_inc(b_in, 16)
            for n in range(B * K + 2, (B + 1) * K):
                load_staged(n)
            sp.wait_ge(b_hi_ready, 1)
            sp.wait_ge(b_lo_ready, 1)
            sp.dma_start(bias_sb[:, :], bias.partition_broadcast(P)).then_inc(bias_in, 16)
            with sp.Fori(0, T - 1) as t:
                sp.wait_ge(summed, T + t + 1)
                sp.dma_start(out_tiles[t], xs[:, t, :]).then_inc(stored, 16)
            for h in range(NH):
                sp.wait_ge(summed, 2 * T + h)
                sp.dma_start(out_tiles[T - 1][:, h * H:(h + 1) * H],
                             xs[:, T - 1, h * H:(h + 1) * H]).then_inc(stored, 16)
            sp.wait_ge(stored, 16 * (T + 1))

        @block.gpsimd
        def _(pool):
            def quantise_x(t):
                pool.wait_ge(q_scaled, t // 2 + 1)
                if t >= 2:
                    pool.wait_ge(x_centred, t - 1)
                nc.gpsimd.tensor_scalar(x_u8[:, t % 2, :], xs[:, t, :], q_scale[:, t:t + 1],
                                        q_bias[:, t:t + 1], ALU.mult, ALU.add).then_inc(x_quantised, 1)

            def centre_ctx(n):
                pool.wait_ge(ctx_quantised, n + 1)
                if n >= K:
                    pool.wait_ge(a2_used, n - K + 1)
                nc.gpsimd.tensor_scalar(a2[:, n % K, :], ctx_u8[:, n % 3, :], -CENTRE, 1.0,
                                        ALU.add, ALU.mult).then_inc(ctx_centred, 1)

            def add_corr(t):
                pool.wait_ge(summed, t + 1)
                pool.wait_ge(corr_ready, t // TB + 1)
                nc.gpsimd.tensor_tensor(xs[:, t, :], xs[:, t, :], corr[:, t // TB, :], ALU.add).then_inc(x1_ready, 1)

            def split_w(k):
                pool.wait_ge(w_hi_ready, k + 1)
                nc.gpsimd.tensor_tensor(w_lo[:, k, :], stage[:, (B * K + k) % RING, :],
                                        w_hi[:, k, :].bitcast(F32), ALU.subtract).then_inc(w_lo_ready[k], 1)

            def add_bias(t):
                pool.wait_ge(y_ready, t + 1)
                nc.gpsimd.tensor_tensor(xs[:, bass.ds(t, 1), :], xs[:, bass.ds(t, 1), :],
                                        bias_sb[:, :].rearrange("p (o n) -> p o n", o=1),
                                        ALU.add).then_inc(bias_added, 1)

            nc.gpsimd.memset(ident[:, :], 0.0).then_inc(ident_ready, 1)
            pool.wait_ge(ident_ready, 1)
            nc.gpsimd.affine_select(out=ident[:, :], in_=ident[:, :], compare_op=ALU.not_equal, fill=1.0,
                                    base=0, pattern=[[-1, P]], channel_multiplier=1).then_inc(ident_ready, 1)
            nc.gpsimd.iota(expert_i[:, :], pattern=[[1, EX], [0, RANK]], base=0,
                           channel_multiplier=0).then_inc(iota_ready, 1)
            def centre(first, last):
                for n in range(first, last + 1):
                    centre_ctx(n)

            centre(0, 5)
            pool.wait_ge(peak_ready, 2)
            nc.gpsimd.partition_all_reduce(peak_all[:, :], peak[:, :], P,
                                           bass.bass_isa.ReduceOp.max).then_inc(peak_all_ready, 1)
            centre(6, 7)
            quantise_x(4)
            quantise_x(5)
            centre(8, 13)
            add_corr(0)
            centre(14, 15)
            add_corr(1)
            for k in range(4):
                split_w(k)
            add_corr(2)
            for k in range(4, K - 1):
                split_w(k)
            add_corr(3)
            pool.wait_ge(bias_in, 16)
            add_bias(0)
            for t in range(4, T):
                add_corr(t)
            with pool.Fori(1, T) as t:
                add_bias(t)

        @block.scalar
        def _(act):
            def centre_x(t):
                act.wait_ge(x_quantised, t + 1)
                if t >= 2:
                    act.wait_ge(a1_transposed, t - 1)
                nc.scalar.activation(a1[:, t % 2, :], x_u8[:, t % 2, :], ACT.Copy, bias=-CENTRE,
                                     accum_out=rowsum[:, t:t + 1]).then_inc(x_centred, 1)

            def quantise_ctx(n):
                act.wait_ge(*staged(n))
                if n >= 3:
                    act.wait_ge(ctx_centred, n - 2)
                nc.scalar.activation(ctx_u8[:, n % 3, :], stage[:, n % RING, :], ACT.Identity,
                                     bias=prm[:, 3:4], scale=inv_s[:, 2:3]).then_inc(ctx_quantised, 1)

            def make_corr(b):
                act.wait_ge(colsum_done, b + 1)
                nc.scalar.activation(corr[:, b, :].rearrange("p (h n) -> p h n", h=NH),
                                     ps[:, COLSUM_BANKS, :], ACT.Identity,
                                     scale=col_scale).then_inc(corr_ready, 1)

            def split_ar():
                act.wait_ge(ar_scaled, 1)
                raw = y[:, :].rearrange("p (k c) -> p k c", c=AR)
                nc.scalar.activation(ar_hi[:, :, 0:ER], raw[:, :, 0:ER], ACT.Identity,
                                     scale=ar_scale[:, 0:1]).then_inc(ar_hi_ready, 1)
                nc.scalar.activation(ar_hi[:, :, ER:AR], raw[:, :, ER:AR], ACT.Identity,
                                     scale=ar_scale[:, 1:2]).then_inc(ar_hi_ready, 1)

            def split_w(k):
                act.wait_ge(*staged(B * K + k))
                nc.scalar.activation(w_hi[:, k, :], stage[:, (B * K + k) % RING, :],
                                     ACT.Copy).then_inc(w_hi_ready, 1)

            def make_y(t, p, first=False):
                act.wait_ge(y_scaled, t + 1)
                if first:
                    act.wait_ge(ar_lo_ready, 2)
                else:
                    act.wait_ge(y_transposed, t)
                nc.scalar.activation(y[:, 0:D], xs[:, t, :], ACT.Identity, bias=y_bias[:, p:p + 1],
                                     scale=y_scale[:, p:p + 1]).then_inc(y_ready, 1)

            def split_yt(t, p, banks):
                act.wait_ge(y_transposed, t + 1)
                nc.scalar.activation(yt_hi[:, p, :, :].rearrange("p (h k) c -> p h (k c)", h=2),
                                     ps[:, banks, :], ACT.Copy).then_inc(yt_hi_ready, 1)
                act.wait_ge(yt_hi_ready, t + 1)
                nc.scalar.activation(yt_hi16[:, :, :], yt_hi[:, p, :, :].bitcast(F32), ACT.Copy,
                                     scale=Y_SCALE).then_inc(yt_hi16_ready, 1)

            def gate_weight(t):
                act.wait_ge(gate_diff, t + 1)
                nc.scalar.activation(gate[:, 1:2], gate[:, 0:1], ACT.Exp,
                                     scale=ar_undo[:, 1:2]).then_inc(gate_exp, 1)

            def split_hct(t):
                act.wait_ge(hc_transposed, t + 1)
                nc.scalar.activation(hct_hi[:, :], ps[:, AR_BANK, HCT], ACT.Copy).then_inc(hct_hi_ready, 1)

            act.wait_ge(ones_ready, 1)
            nc.scalar.activation(gate[:, 0:1], ones16[:, 0:1], ACT.Copy)
            act.wait_ge(consts_ready, 1)
            act.wait_ge(quant_in, 16)
            def quantise(first, last):
                for n in range(first, last + 1):
                    quantise_ctx(n)

            quantise(0, 1)
            centre_x(0)
            centre_x(1)
            quantise(2, 5)
            centre_x(2)
            quantise_ctx(6)
            centre_x(3)
            quantise_ctx(7)
            quantise_ctx(8)
            make_corr(0)
            quantise_ctx(9)
            split_ar()
            centre_x(4)
            centre_x(5)
            quantise(10, 14)
            centre_x(6)
            quantise_ctx(15)
            centre_x(7)
            for k in range(3):
                split_w(k)
            make_corr(1)
            make_y(0, 0, first=True)
            split_w(3)
            split_yt(0, 0, yt_banks(0))
            act.wait_ge(b_in, 16)
            nc.scalar.activation(b_hi[:, :], bias_sb[:, :], ACT.Copy).then_inc(b_hi_ready, 1)
            split_w(4)
            split_w(5)
            split_w(6)
            gate_weight(0)
            split_w(7)
            make_y(1, 1)
            split_hct(0)
            split_yt(1, 1, yt_banks(1))

            def tile(t, p):
                make_y(t + 1, 1 - p)
                gate_weight(t)
                split_hct(t)
                split_yt(t + 1, 1 - p, yt_banks(1))

            with act.Fori(0, (T - 2) // 2) as i:
                tile(2 * i + 1, 1)
                tile(2 * i + 2, 0)
            gate_weight(T - 1)
            split_hct(T - 1)

        @block.vector
        def _(dve):
            steps = [0]

            def then(ins):
                steps[0] += 1
                ins.then_inc(vec_step, 1)
                dve.wait_ge(vec_step, steps[0])

            LN_LINKS = 13

            def statistics(t, p):
                nc.vector.bn_stats(bn[:, p, 0, :], xs[:, t, 0:H])
                return nc.vector.bn_stats(bn[:, p, 1, :], xs[:, t, H:D])

            def layernorm_steps(p, n, link):
                nc.vector.memset(wait_pad[:, :], 0.0)
                for j in range(n):
                    last = nc.vector.bn_aggr(mv[:, p + j, :], bn[:, p + j, :, :].rearrange("p a b -> p (a b)"))
                link(last)
                var = mv[:, p:p + n, 1]
                half, v, g, f, r = (rsq[:, i, p:p + n] for i in range(5))
                nc.vector.tensor_scalar(half, var, EPS, 0.5, ALU.add, ALU.mult)
                link(nc.vector.tensor_scalar(v, var, EPS, None, ALU.add))
                link(nc.vector.tensor_scalar(v.bitcast(I32), v.bitcast(I32), 1, None, ALU.logical_shift_right))
                link(nc.vector.tensor_scalar(r.bitcast(I32), v.bitcast(I32), -1.0, RSQRT_SEED,
                                             ALU.mult, ALU.add))
                link(nc.vector.tensor_tensor(g, half, r, ALU.mult))
                link(nc.vector.tensor_tensor(f, g, r, ALU.mult))
                nc.vector.scalar_tensor_tensor(out=g, in0=f, scalar=-1.5, in1=g, op0=ALU.add, op1=ALU.mult)
                link(nc.vector.scalar_tensor_tensor(out=r, in0=f, scalar=-1.5, in1=r, op0=ALU.add, op1=ALU.mult))
                link(nc.vector.tensor_tensor(f, g, r, ALU.mult))
                link(nc.vector.scalar_tensor_tensor(out=r, in0=f, scalar=-1.5, in1=r, op0=ALU.add, op1=ALU.mult))
                link(nc.vector.tensor_tensor(f, r, r, ALU.mult))
                link(nc.vector.tensor_tensor(f, f, half, ALU.mult))
                link(nc.vector.scalar_tensor_tensor(out=r, in0=f, scalar=-1.5, in1=r, op0=ALU.add, op1=ALU.mult))
                return r

            def statistics_x(t):
                dve.wait_ge(x_in[t], 16)
                statistics(t, t % 2).then_inc(x_statistics, 1)

            def scale_x(t):
                dve.wait_ge(x_statistics, t + 2)
                minus_r = layernorm_steps(0, 2, then)
                nc.vector.tensor_scalar(q_scale[:, t:t + 2], minus_r, -1.0, inv_s[:, 0:1], ALU.mult, ALU.mult)
                then(nc.vector.tensor_tensor(rsq[:, 5, :], mv[:, :, 0], minus_r, ALU.mult))
                nc.vector.tensor_scalar(q_bias[:, t:t + 2], rsq[:, 5, :], inv_s[:, 0:1], prm[:, 1:2],
                                        ALU.mult, ALU.add).then_inc(q_scaled, 1)

            def quantise_x(t):
                dve.wait_ge(q_scaled, t // 2 + 1)
                if t >= 2:
                    dve.wait_ge(x_centred, t - 1)
                nc.vector.tensor_scalar(x_u8[:, t % 2, :], xs[:, t, :], q_scale[:, t:t + 1],
                                        q_bias[:, t:t + 1], ALU.mult, ALU.add).then_inc(x_quantised, 1)

            def take_a1t(t):
                dve.wait_ge(a1_transposed, t + 1)
                if t >= 4:
                    dve.wait_ge(stage1_done, t - 3)
                nc.vector.tensor_copy(a1_t[:, t % 4, :, :].rearrange("p k c -> p (k c)"),
                                      ps[:, a1_bank(t), :].bitcast(BF16)).then_inc(a1t_ready, 1)

            def sum_x1(t):
                dve.wait_ge(stage1_done, t + 1)
                dve.wait_ge(x_quantised, t + 1)
                nc.vector.scalar_tensor_tensor(
                    out=xs[:, t, :].rearrange("p (h n) -> p h n", h=NH),
                    in0=ps[:, s1_bank(t):s1_bank(t) + 2, :], scalar=s12,
                    in1=xs[:, t, :].rearrange("p (h n) -> p h n", h=NH),
                    op0=ALU.mult, op1=ALU.add).then_inc(summed, 1)

            def make_row_term(t):
                dve.wait_ge(x_centred, t + 1)
                nc.vector.tensor_scalar(row_term[:, t:t + 1], rowsum[:, t:t + 1], k_d1, row_scale,
                                        ALU.add, ALU.mult).then_inc(row_ready, 1)

            def scale_y(t, p):
                n = [0]

                def link(ins):
                    n[0] += 1
                    ins.then_inc(ln_step, 1)
                    dve.wait_ge(ln_step, (t - 2) * LN_LINKS + n[0])

                dve.wait_ge(x1_ready, t + 1)
                dve.wait_ge(y_ready, t - 1)
                link(statistics(t, p))
                minus_r = layernorm_steps(p, 1, link)
                assert n[0] == LN_LINKS, n
                nc.vector.tensor_scalar(y_scale[:, p:p + 1], minus_r, -1.0, None, ALU.mult)
                nc.vector.tensor_tensor(y_bias[:, p:p + 1], mv[:, p, 0:1], minus_r,
                                        ALU.mult).then_inc(y_scaled, 1)

            def scale_first_ys():
                dve.wait_ge(x1_ready, 2)
                statistics(0, 0)
                then(statistics(1, 1))
                minus_r = layernorm_steps(0, 2, then)
                nc.vector.tensor_scalar(y_scale[:, :], minus_r, -1.0, None, ALU.mult)
                nc.vector.tensor_tensor(y_bias[:, :], mv[:, :, 0], minus_r, ALU.mult).then_inc(y_scaled, 2)

            def find_peaks():
                dve.wait_ge(ar_in, 16)
                raw = y[:, :].rearrange("p (k c) -> p k c", c=AR)
                nc.vector.tensor_reduce(peak[:, 0:1], raw[:, :, 0:ER], mybir.AxisListType.XY, ALU.max,
                                        apply_absolute_value=True).then_inc(peak_ready, 1)
                nc.vector.tensor_reduce(peak[:, 1:2], raw[:, :, ER:AR], mybir.AxisListType.XY, ALU.max,
                                        apply_absolute_value=True).then_inc(peak_ready, 1)

            def scale_ar():
                dve.wait_ge(peak_all_ready, 1)
                then(nc.vector.tensor_scalar(peak_all[:, :], peak_all[:, :], AR_FLOOR, None, ALU.max))
                then(nc.vector.tensor_scalar(peak_all[:, :].bitcast(I32), peak_all[:, :].bitcast(I32),
                                             EXPONENT, None, ALU.bitwise_and))
                nc.vector.tensor_scalar(ar_undo[:, :], peak_all[:, :], 1.0 / Y_SCALE, None, ALU.mult)
                then(nc.vector.reciprocal(ar_scale[:, :], peak_all[:, :]))
                nc.vector.tensor_scalar(den_scale, ar_scale[:, 0:1], Y_SCALE / SCALING, None,
                                        ALU.mult).then_inc(ar_scaled, 1)

            def split_ar():
                dve.wait_ge(ar_hi_ready, 2)
                raw = y[:, :].rearrange("p (k c) -> p k c", c=AR)
                for cols, i in ((slice(0, ER), 0), (slice(ER, AR), 1)):
                    nc.vector.scalar_tensor_tensor(out=ar_lo[:, :, cols], in0=raw[:, :, cols],
                                                   scalar=ar_scale[:, i:i + 1], in1=ar_hi[:, :, cols],
                                                   op0=ALU.mult, op1=ALU.subtract).then_inc(ar_lo_ready, 1)

            def split_w(k):
                dve.wait_ge(w_hi_ready, k + 1)
                nc.vector.tensor_tensor(w_lo[:, k, :], stage[:, (B * K + k) % RING, :],
                                        w_hi[:, k, :].bitcast(F32), ALU.subtract).then_inc(w_lo_ready[k], 1)

            def split_yt(t, p, banks):
                def halves(a):
                    return a.rearrange("p (h k) c -> p h (k c)", h=2)

                dve.wait_ge(yt_hi_ready, t + 1)
                nc.vector.tensor_tensor(halves(yt_lo[:, p, :, :]), ps[:, banks, :],
                                        halves(yt_hi[:, p, :, :].bitcast(F32)),
                                        ALU.subtract).then_inc(yt_lo_ready, 1)
                dve.wait_ge(yt_hi16_ready, t + 1)
                nc.vector.scalar_tensor_tensor(out=halves(yt_lo16[:, :, :]), in0=ps[:, banks, :],
                                               scalar=Y_SCALE, in1=halves(yt_hi16[:, :, :]),
                                               op0=ALU.mult, op1=ALU.subtract).then_inc(yt_lo16_ready, 1)

            GATE_LINKS = 8

            def gate_tile(t):
                n = [0]

                def link(ins):
                    n[0] += 1
                    ins.then_inc(gate_step, 1)
                    dve.wait_ge(gate_step, t * GATE_LINKS + n[0])

                logits = ps[:, AR_BANK, ER:AR]
                dve.wait_ge(ar_done, t + 1)
                nc.vector.memset(wait_pad[:, :], 0.0)
                link(nc.vector.max(top[:, :], logits))
                nc.vector.tensor_tensor(gate[:, 0:1], top[:, 1:2], top[:, 0:1], ALU.subtract).then_inc(gate_diff, 1)
                link(nc.vector.max_index(top_i[:, :], top[:, :], logits))
                link(nc.vector.tensor_copy(top_f[:, :], top_i[:, :]))
                dve.wait_ge(gate_exp, t + 1)
                link(nc.vector.tensor_scalar(gate[:, 2:3], gate[:, 1:2], 1.0, den_scale, ALU.add, ALU.mult))
                link(nc.vector.reciprocal(gate[:, 3:4], gate[:, 2:3]))
                link(nc.vector.tensor_scalar(gate[:, 4:5], gate[:, 1:2], gate[:, 3:4], None, ALU.mult))
                nc.vector.tensor_scalar(c1[:, :], expert[:, :], top_f[:, 0:1], gate[:, 3:4],
                                        ALU.is_equal, ALU.mult)
                link(nc.vector.tensor_scalar(c2[:, :], expert[:, :], top_f[:, 1:2], gate[:, 4:5],
                                             ALU.is_equal, ALU.mult))
                link(nc.vector.tensor_tensor(cw[:, :], c1[:, :], c2[:, :], ALU.add))
                nc.vector.tensor_tensor(hc[:, :], ps[:, AR_BANK, 0:ER], cw[:, :],
                                        ALU.mult).then_inc(hc_ready, 1)
                assert n[0] == GATE_LINKS

            def split_hct(t):
                dve.wait_ge(hct_hi_ready, t + 1)
                nc.vector.tensor_tensor(hct_lo[:, :], ps[:, AR_BANK, HCT], hct_hi[:, :].bitcast(F32),
                                        ALU.subtract).then_inc(hct_lo_ready, 1)

            def sum_out(t, p, h0, h1):
                nc.vector.scalar_tensor_tensor(
                    out=xs[:, t, h0 * H:h1 * H].rearrange("p (h n) -> p h n", n=H),
                    in0=ps[:, OUT_BANK[p] + h0:OUT_BANK[p] + h1, :],
                    scalar=row_term[:, bass.ds(t, 1)],
                    in1=xs[:, t, h0 * H:h1 * H].rearrange("p (h n) -> p h n", n=H),
                    op0=ALU.add, op1=ALU.add).then_inc(summed, 1)

            nc.vector.memset(ones16[:, :], 1.0).then_inc(ones_ready, 1)
            dve.wait_ge(quant_in, 16)
            nc.vector.reciprocal(inv_s[:, 0:1], prm[:, 0:1])
            then(nc.vector.reciprocal(inv_s[:, 2:3], prm[:, 2:3]))
            nc.vector.tensor_tensor(s12, prm[:, 0:1], prm[:, 2:3], ALU.mult)
            nc.vector.tensor_scalar(d1, prm[:, 1:2], -1.0, CENTRE, ALU.mult, ALU.add)
            then(nc.vector.tensor_scalar(d2, prm[:, 3:4], -1.0, CENTRE, ALU.mult, ALU.add))
            nc.vector.tensor_tensor(col_scale, d1, s12, ALU.mult)
            nc.vector.tensor_tensor(row_scale, d2, s12, ALU.mult)
            nc.vector.tensor_scalar(k_d1, d1, float(D), None, ALU.mult).then_inc(consts_ready, 1)
            dve.wait_ge(consts_ready, 1)
            dve.wait_ge(ident_ready, 2)
            nc.vector.tensor_copy(ident16[:, :], ident[:, :]).then_inc(ident16_ready, 1)
            dve.wait_ge(iota_ready, 1)
            then(nc.vector.tensor_copy(expert[:, :], expert_i[:, :]))
            statistics_x(0)
            statistics_x(1)
            scale_x(0)
            quantise_x(0)
            quantise_x(1)
            statistics_x(2)
            take_a1t(0)
            take_a1t(1)
            statistics_x(3)
            scale_x(2)
            quantise_x(2)
            quantise_x(3)
            find_peaks()
            scale_ar()
            take_a1t(2)
            statistics_x(4)
            take_a1t(3)
            statistics_x(5)
            scale_x(4)
            sum_x1(0)
            sum_x1(1)
            statistics_x(6)
            take_a1t(4)
            take_a1t(5)
            statistics_x(7)
            scale_x(6)
            quantise_x(6)
            sum_x1(2)
            quantise_x(7)
            sum_x1(3)
            take_a1t(6)
            take_a1t(7)
            split_ar()
            scale_first_ys()
            sum_x1(4)
            sum_x1(5)
            split_yt(0, 0, yt_banks(0))
            for t in range(T):
                make_row_term(t)
            dve.wait_ge(b_hi_ready, 1)
            nc.vector.tensor_tensor(b_lo[:, :], bias_sb[:, :], b_hi[:, :].bitcast(F32),
                                    ALU.subtract).then_inc(b_lo_ready, 1)
            sum_x1(6)
            gate_tile(0)
            sum_x1(7)
            scale_y(2, 0)
            split_hct(0)
            split_w(7)
            dve.wait_ge(row_ready, T)
            split_yt(1, 1, yt_banks(1))

            def tile(t, p, scale=True, split=True):
                gate_tile(t)
                split_hct(t)
                dve.wait_ge(out_done, t)
                dve.wait_ge(bias_added, t)
                sum_out(t - 1, 1 - p, 0, NH)
                if scale:
                    scale_y(t + 2, p)
                if split:
                    split_yt(t + 1, 1 - p, yt_banks(1))

            with dve.Fori(0, (T - 4) // 2) as i:
                tile(2 * i + 1, 1)
                tile(2 * i + 2, 0)
            tile(T - 3, 1)
            tile(T - 2, 0, scale=False)
            tile(T - 1, 1, scale=False, split=False)
            dve.wait_ge(bias_added, T)
            for h in range(NH):
                dve.wait_ge(out_done, T + h)
                sum_out(T - 1, 1, h, h + 1)

        @block.tensor
        def _(pe):
            def transpose_a1(t):
                pe.wait_ge(x_centred, t + 1)
                if t >= 4:
                    pe.wait_ge(summed, t - 3)
                bank = ps[:, a1_bank(t), :].bitcast(BF16)
                for k in range(K):
                    last = nc.tensor.transpose(bank[:, k * P:(k + 1) * P], a1[:, t % 2, k * P:(k + 1) * P],
                                               ident16[:, :])
                last.then_inc(a1_transposed, 1)

            def stage1(q, between, colsum_from=0):
                b, first = q // PPB, q % PPB == 0
                def product(k, t):
                    pe.wait_ge(ctx_centred, b * K + k + 1)
                    for h in range(NH):
                        ins = nc.tensor.matmul(ps[:, s1_bank(t) + h, :], a1_t[:, t % 4, k, :],
                                               a2[:, k, h * H:(h + 1) * H], start=k == 0, stop=k == K - 1)
                    if k == K - 1:
                        ins.then_inc(stage1_done, 1)
                    return ins

                ahead = 0 if first else 4
                pe.wait_ge(a1t_ready, 2 * q + 2)
                for k in range(ahead):
                    product(k, 2 * q)
                if not first:
                    pe.wait_ge(corr_ready, b + 1)
                for k in range(K):
                    if k >= ahead:
                        product(k, 2 * q)
                    last = product(k, 2 * q + 1)
                    if not first and k < K - 1:
                        last.then_inc(a2_used, 1)
                    if k in between:
                        between[k]()
                    if first and k >= colsum_from:
                        for kk in range(0 if k == colsum_from else k, k + 1):
                            for h in range(NH):
                                last = nc.tensor.matmul(ps[:, COLSUM_BANKS.start + h, :], ones16[:, 0:P],
                                                        a2[:, kk, h * H:(h + 1) * H],
                                                        start=kk == 0, stop=kk == K - 1)
                        if k == K - 1:
                            last.then_inc(colsum_done, 1)
                if not first:
                    nc.tensor.ldweights(ident16[:, :]).then_inc(a2_used, 1)

            def transpose_y(t, banks):
                pe.wait_ge(y_ready, t + 1)
                for k in range(K):
                    last = nc.tensor.transpose(ps[:, banks.start + k // 4, (k % 4) * P:(k % 4 + 1) * P],
                                               y[:, k * P:(k + 1) * P], ident[:, :])
                last.then_inc(y_transposed, 1)

            def transpose_hc(t):
                pe.wait_ge(hc_ready, t + 1)
                nc.tensor.transpose(ps[:, AR_BANK, HCT], hc[:, :], ident[:, :]).then_inc(hc_transposed, 1)

            def narrow(t):
                pe.wait_ge(yt_hi16_ready, t + 1)
                dst = ps[:, AR_BANK, 0:AR]
                for k in range(K):
                    nc.tensor.matmul(dst, yt_hi16[:, k, :], ar_hi[:, k, :], start=k == 0, stop=False)
                    nc.tensor.matmul(dst, yt_hi16[:, k, :], ar_lo[:, k, :], start=False, stop=False)
                pe.wait_ge(yt_lo16_ready, t + 1)
                for k in range(K):
                    last = nc.tensor.matmul(dst, yt_lo16[:, k, :], ar_hi[:, k, :], start=False, stop=k == K - 1)
                last.then_inc(ar_done, 1)

            def lora(t, p):
                pe.wait_ge(hct_lo_ready, t + 1)
                for part, rhs in ((hct_hi, b_hi), (hct_hi, b_lo), (hct_lo, b_hi)):
                    for h in range(NH):
                        nc.tensor.matmul(ps[:, OUT_BANK[p] + h, :], part[:, :], rhs[:, h * H:(h + 1) * H],
                                         start=False, stop=False)

            def main(t, p, between, first=False, last=False):
                out_ps = OUT_BANK[p]
                pe.wait_ge(yt_lo_ready, t + 1)
                for k in range(K):
                    if first:
                        pe.wait_ge(w_lo_ready[k], 1)
                    hi, lo = yt_hi[:, p, k, :], yt_lo[:, p, k, :]
                    start, stop = k == 0, k == K - 1
                    for part, rhs in ((hi, w_hi), (hi, w_lo), (lo, w_hi)):
                        for h in range(NH):
                            ins = nc.tensor.matmul(ps[:, out_ps + h, :], part, rhs[:, k, h * H:(h + 1) * H],
                                                   start=start and part is hi and rhs is w_hi,
                                                   stop=stop and part is lo)
                            if stop and part is lo and (last or h == NH - 1):
                                ins.then_inc(out_done, 1)
                    if k in between:
                        between[k]()

            pe.wait_ge(ones_ready, 1)
            pe.wait_ge(x_in[0], 16)
            for _ in range(WARM_UP):
                nc.tensor.matmul(ps[:, COLSUM_BANKS.start, 0:3 * P], ones16[:, 0:P], ones16[:, :],
                                 start=True, stop=True)
            pe.wait_ge(ident16_ready, 1)
            transpose_a1(0)
            transpose_a1(1)
            stage1(0, {5: lambda: transpose_a1(2), 6: lambda: transpose_a1(3)})
            stage1(1, {5: lambda: transpose_a1(4), 6: lambda: transpose_a1(5)})
            stage1(2, {5: lambda: transpose_a1(6), 6: lambda: transpose_a1(7)}, colsum_from=7)
            pe.wait_ge(ident_ready, 2)

            def first_y():
                pe.wait_ge(summed, TB + 1)
                transpose_y(0, yt_banks(0))
            stage1(3, {5: first_y})

            def second_y():
                pe.wait_ge(summed, T)
                transpose_y(1, yt_banks(1))

            pe.wait_ge(ar_lo_ready, 2)
            pe.wait_ge(summed, TB + 2)
            narrow(0)
            main(0, 0, {3: lambda: transpose_hc(0), 5: second_y,
                        6: lambda: (pe.wait_ge(b_lo_ready, 1), lora(0, 0))}, first=True)

            def tile(t, p):
                narrow(t)
                pe.wait_ge(summed, T + t - 1)
                main(t, p, {2: lambda: transpose_hc(t), 3: lambda: transpose_y(t + 1, yt_banks(1)),
                            5: lambda: lora(t, p)})

            with pe.Fori(0, (T - 2) // 2) as i:
                tile(2 * i + 1, 1)
                tile(2 * i + 2, 0)
            last = T - 1
            narrow(last)
            pe.wait_ge(summed, T + last - 1)
            main(last, 1, {2: lambda: transpose_hc(last), 5: lambda: lora(last, 1)}, last=True)


def kernel(x, ctx_4096, L0_xattn_x1_scale, L0_xattn_x1_zp, L0_xattn_x2_scale, L0_xattn_x2_zp,
           L0_ffn_W_base, L0_ffn_b_base, L0_ffn_W_router, L0_ffn_A_stack, L0_ffn_B_stack):
    import numpy as np
    import concourse.bacc as bacc
    from concourse.bass_utils import run_bass_kernel_spmd as run

    D = x.shape[-1]
    experts, rank, _ = L0_ffn_A_stack.shape
    ar = np.concatenate([np.reshape(L0_ffn_A_stack, (experts * rank, D)), np.asarray(L0_ffn_W_router)])
    ar = np.transpose(np.reshape(ar.T, (D // P, P, experts * rank + experts)), (1, 0, 2))
    arrays = {
        "x": x, "ctx_kv": ctx_4096,
        "quant": np.concatenate([np.reshape(v, (1,)) for v in (L0_xattn_x1_scale, L0_xattn_x1_zp,
                                                               L0_xattn_x2_scale, L0_xattn_x2_zp)]),
        "w_t": np.transpose(L0_ffn_W_base), "bias": L0_ffn_b_base,
        "ar_t": np.reshape(ar, (P, -1)),
        "b_t": np.reshape(np.transpose(L0_ffn_B_stack, (0, 2, 1)), (experts * rank, D)),
    }
    arrays = {name: np.ascontiguousarray(a) for name, a in arrays.items()}
    nc = bacc.Bacc("TRN2", target_bir_lowering=False, num_devices=1)
    args = {name: nc.dram_tensor(f"in_{name}", a.shape, mybir.dt.from_np(a.dtype), kind="ExternalInput").ap()
            for name, a in arrays.items()}
    args["out"] = nc.dram_tensor("out_dram", x.shape, F32, kind="ExternalOutput").ap()
    xattn_ffn(nc, **args)
    result = run(nc, [{f"in_{name}": a for name, a in arrays.items()}], core_ids=[0])
    return result.results[0]["out_dram"]
```

```python
from contextlib import ExitStack

import concourse.bass as bass
from concourse import mybir

P = 128
ALU = mybir.AluOpType
ACT = mybir.ActivationFunctionType
F32 = mybir.dt.float32
F32R = mybir.dt.float32r
F16 = mybir.dt.float16
BF16 = mybir.dt.bfloat16
U8 = mybir.dt.uint8
I32 = mybir.dt.int32
U32 = mybir.dt.uint32

CENTRE = 128.0
EPS = 1e-5
Y_SCALE = 1024.0
AR_SCALE = 2.0 ** 14
AR_FLOOR = 1e-30
EXPONENT = 0x7F800000
RSQRT_SEED = float(0x5F3759DF)
SCALING = 2.0


def xattn_ffn(nc, x, ctx_kv, quant, w_t, bias, ar_t, b_t, out):
    B, S, D = x.shape
    T = B * S // P
    TB = T // B
    K = D // P
    ER = b_t.shape[0]
    EX = 8
    RANK = ER // EX
    AR = ar_t.shape[1] // K
    H = 512
    NH = D // H
    WARM_UP = 24
    RING = 6
    PAIRS = T // 2
    PPB = TB // 2
    assert ER == P and AR == ER + EX and NH == 2 and D == ctx_kv.shape[1]

    x_tiles = x.rearrange("b (t p) d -> (b t) p d", p=P)
    out_tiles = out.rearrange("b (t p) d -> (b t) p d", p=P)
    ctx_tiles = ctx_kv.rearrange("b (k p) n -> (b k) p n", p=P)
    w_tiles = w_t.rearrange("(k p) n -> k p n", p=P)

    with ExitStack() as stack:
        def sb(name, shape, dt):
            return stack.enter_context(nc.sbuf_tensor(name, shape, dt))

        def sem(name):
            return stack.enter_context(nc.semaphore(name))

        xs = sb("xs", [P, T, D], F32)
        stage = sb("stage", [P, RING, D], F32)
        ctx_u8 = sb("ctx_u8", [P, 3, D], U8)
        a2 = sb("a2", [P, K, D], BF16)
        x_u8 = sb("x_u8", [P, 2, D], U8)
        a1 = sb("a1", [P, 2, D], BF16)
        a1_t = sb("a1_t", [P, 4, K, P], BF16)
        corr = sb("corr", [P, B, D], F32)
        bias_sb = sb("bias_sb", [P, D], F32)
        w_hi = sb("w_hi", [P, K, D], F32R)
        w_lo = sb("w_lo", [P, K, D], F32R)
        ar_hi = sb("ar_hi", [P, K, AR], F16)
        ar_lo = sb("ar_lo", [P, K, AR], F16)
        b_hi = sb("b_hi", [P, D], F32R)
        b_lo = sb("b_lo", [P, D], F32R)
        y = sb("y", [P, K * AR], F32)
        yt_hi = sb("yt_hi", [P, 2, K, P], F32R)
        yt_lo = sb("yt_lo", [P, 2, K, P], F32R)
        yt_hi16 = sb("yt_hi16", [P, K, P], F16)
        yt_lo16 = sb("yt_lo16", [P, K, P], F16)
        hc = sb("hc", [P, ER], F32)
        hct_hi = sb("hct_hi", [P, P], F32R)
        hct_lo = sb("hct_lo", [P, P], F32R)
        ident = sb("ident", [P, P], F32)
        ident16 = sb("ident16", [P, P], BF16)
        ones16 = sb("ones16", [P, 3 * P], BF16)
        expert_i = sb("expert_i", [P, ER], I32)
        expert = sb("expert", [P, ER], F32)
        prm = sb("prm", [P, 4], F32)
        inv_s = sb("inv_s", [P, 4], F32)
        con = sb("con", [P, 8], F32)
        bn = sb("bn", [P, 2, 2, 6], F32)
        mv = sb("mv", [P, 2, 2], F32)
        rsq = sb("rsq", [P, 6, 2], F32)
        peak = sb("peak", [P, 2], F32)
        peak_all = sb("peak_all", [P, 2], F32)
        ar_scale = sb("ar_scale", [P, 2], F32)
        ar_undo = sb("ar_undo", [P, 2], F32)
        q_scale = sb("q_scale", [P, T], F32)
        q_bias = sb("q_bias", [P, T], F32)
        rowsum = sb("rowsum", [P, T], F32)
        row_term = sb("row_term", [P, T], F32)
        y_scale = sb("y_scale", [P, 2], F32)
        y_bias = sb("y_bias", [P, 2], F32)
        wait_pad = sb("wait_pad", [P, 1], F32)
        top = sb("top", [P, 8], F32)
        top_i = sb("top_i", [P, 8], U32)
        top_f = sb("top_f", [P, 8], F32)
        gate = sb("gate", [P, 8], F32)
        c1 = sb("c1", [P, ER], F32)
        c2 = sb("c2", [P, ER], F32)
        cw = sb("cw", [P, ER], F32)
        ps = stack.enter_context(nc.psum_tensor("ps", [P, 8, H], F32))

        s12, d1, d2, col_scale, row_scale, k_d1, den_scale = (con[:, i:i + 1] for i in range(7))

        def s1_bank(t):
            return 4 * (t // 2 % 2) + 2 * (t % 2)

        def a1_bank(t):
            return 4 * (t // 2 % 2) + t % 2

        COLSUM_BANKS = slice(6, 8)
        OUT_BANK = [0, 4]
        AR_BANK = 2
        LAST_PIECES = ((0, H), (H, H + H // 2), (H + H // 2, D))
        HCT = slice(256, 256 + P)

        def yt_banks(t):
            return slice(2, 4) if t == 0 else slice(6, 8)

        quant_in = sem("quant_in")
        x_in = [sem(f"x_in{t}") for t in range(T)]
        stage_in = [sem(f"stage_in{r}") for r in range(RING)]
        ar_in, b_in, bias_in = sem("ar_in"), sem("b_in"), sem("bias_in")
        stored = sem("stored")
        ident_ready, iota_ready = sem("ident_ready"), sem("iota_ready")
        ident16_ready, ones_ready = sem("ident16_ready"), sem("ones_ready")
        consts_ready = sem("consts_ready")
        vec_step = sem("vec_step")
        x_statistics = sem("x_statistics")
        q_scaled = sem("q_scaled")
        x_quantised = sem("x_quantised")
        x_centred = sem("x_centred")
        a1_transposed = sem("a1_transposed")
        a1t_ready = sem("a1t_ready")
        ctx_quantised = sem("ctx_quantised")
        ctx_centred = sem("ctx_centred")
        a2_used = sem("a2_used")
        stage1_done = sem("stage1_done")
        summed = sem("summed")
        colsum_done = sem("colsum_done")
        corr_ready = sem("corr_ready")
        x1_ready = sem("x1_ready")
        row_ready = sem("row_ready")
        w_hi_ready = sem("w_hi_ready")
        w_lo_ready = [sem(f"w_lo_ready{k}") for k in range(K)]
        peak_ready, peak_all_ready = sem("peak_ready"), sem("peak_all_ready")
        ar_scale_ready, ar_scaled = sem("ar_scale_ready"), sem("ar_scaled")
        ar_hi_ready, ar_lo_ready = sem("ar_hi_ready"), sem("ar_lo_ready")
        b_hi_ready, b_lo_ready = sem("b_hi_ready"), sem("b_lo_ready")
        ln_step = sem("ln_step")
        y_scaled = sem("y_scaled")
        y_ready = sem("y_ready")
        y_transposed = sem("y_transposed")
        yt_hi_ready, yt_lo_ready = sem("yt_hi_ready"), sem("yt_lo_ready")
        first_half_hi, first_half_lo = sem("first_half_hi"), sem("first_half_lo")
        yt_hi16_ready, yt_lo16_ready = sem("yt_hi16_ready"), sem("yt_lo16_ready")
        ar_done = sem("ar_done")
        gate_step = sem("gate_step")
        gate_diff = sem("gate_diff")
        gate_exp = sem("gate_exp")
        hc_ready = sem("hc_ready")
        hc_transposed = sem("hc_transposed")
        hct_hi_ready, hct_lo_ready = sem("hct_hi_ready"), sem("hct_lo_ready")
        out_done = sem("out_done")
        bias_added = sem("bias_added")

        def staged(n):
            return stage_in[n % RING], 16 * (n // RING + 1)

        block = stack.enter_context(nc.Block())

        @block.sync
        def _(sp):
            def load_x(t):
                sp.dma_start(xs[:, t, :], x_tiles[t]).then_inc(x_in[t], 16)

            def load_staged(n):
                if n >= RING:
                    m = n - RING
                    if m < B * K:
                        sp.wait_ge(ctx_quantised, m + 1)
                    else:
                        sp.wait_ge(w_hi_ready, m - B * K + 1)
                        sp.wait_ge(w_lo_ready[m - B * K], 1)
                src = ctx_tiles[n] if n < B * K else w_tiles[n - B * K]
                sp.dma_start(stage[:, n % RING, :], src).then_inc(stage_in[n % RING], 16)

            sp.dma_start(prm[:, :], quant.partition_broadcast(P)).then_inc(quant_in, 16)
            load_x(0)
            load_x(1)
            load_staged(0)
            load_staged(1)
            load_x(2)
            load_x(3)
            for n in range(2, K - 1):
                load_staged(n)
            sp.dma_start(y[:, :], ar_t).then_inc(ar_in, 16)
            load_staged(K - 1)
            load_x(4)
            load_x(5)
            load_staged(K)
            load_staged(K + 1)
            load_x(6)
            load_x(7)
            for n in range(K + 2, B * K + 2):
                load_staged(n)
            sp.dma_start(bias_sb[:, :], b_t).then_inc(b_in, 16)
            for n in range(B * K + 2, (B + 1) * K):
                load_staged(n)
            sp.wait_ge(b_hi_ready, 1)
            sp.wait_ge(b_lo_ready, 1)
            sp.dma_start(bias_sb[:, :], bias.partition_broadcast(P)).then_inc(bias_in, 16)
            with sp.Fori(0, T - 1) as t:
                sp.wait_ge(summed, T + t + 1)
                sp.dma_start(out_tiles[t], xs[:, t, :]).then_inc(stored, 16)
            for i, (start, end) in enumerate(LAST_PIECES):
                sp.wait_ge(summed, 2 * T + i)
                sp.dma_start(out_tiles[T - 1][:, start:end], xs[:, T - 1, start:end]).then_inc(stored, 16)
            sp.wait_ge(stored, 16 * (T - 1 + len(LAST_PIECES)))

        @block.gpsimd
        def _(pool):
            def quantise_x(t):
                pool.wait_ge(q_scaled, t // 2 + 1)
                if t >= 2:
                    pool.wait_ge(x_centred, t - 1)
                nc.gpsimd.tensor_scalar(x_u8[:, t % 2, :], xs[:, t, :], q_scale[:, t:t + 1],
                                        q_bias[:, t:t + 1], ALU.mult, ALU.add).then_inc(x_quantised, 1)

            def centre_ctx(n):
                pool.wait_ge(ctx_quantised, n + 1)
                if n >= K:
                    pool.wait_ge(a2_used, n - K + 1)
                nc.gpsimd.tensor_scalar(a2[:, n % K, :], ctx_u8[:, n % 3, :], -CENTRE, 1.0,
                                        ALU.add, ALU.mult).then_inc(ctx_centred, 1)

            def add_corr(t):
                pool.wait_ge(summed, t + 1)
                pool.wait_ge(corr_ready, t // TB + 1)
                nc.gpsimd.tensor_tensor(xs[:, t, :], xs[:, t, :], corr[:, t // TB, :], ALU.add).then_inc(x1_ready, 1)

            def apply_ar_scale():
                pool.wait_ge(ar_scale_ready, 1)
                raw = y[:, :].rearrange("p (k c) -> p k c", c=AR)
                for cols, i in ((slice(0, ER), 0), (slice(ER, AR), 1)):
                    nc.gpsimd.tensor_scalar(raw[:, :, cols], raw[:, :, cols], ar_scale[:, i:i + 1], 0.0,
                                            ALU.mult, ALU.add).then_inc(ar_scaled, 1)

            def split_ar():
                pool.wait_ge(ar_hi_ready, 1)
                nc.gpsimd.tensor_tensor(ar_lo[:, :, :].rearrange("p k c -> p (k c)"), y[:, :],
                                        ar_hi[:, :, :].rearrange("p k c -> p (k c)"),
                                        ALU.subtract).then_inc(ar_lo_ready, 1)

            def split_w(k):
                pool.wait_ge(w_hi_ready, k + 1)
                nc.gpsimd.tensor_tensor(w_lo[:, k, :], stage[:, (B * K + k) % RING, :],
                                        w_hi[:, k, :].bitcast(F32), ALU.subtract).then_inc(w_lo_ready[k], 1)

            def add_bias(t):
                pool.wait_ge(y_ready, t + 1)
                nc.gpsimd.tensor_tensor(xs[:, bass.ds(t, 1), :], xs[:, bass.ds(t, 1), :],
                                        bias_sb[:, :].rearrange("p (o n) -> p o n", o=1),
                                        ALU.add).then_inc(bias_added, 1)

            nc.gpsimd.memset(ident[:, :], 0.0).then_inc(ident_ready, 1)
            pool.wait_ge(ident_ready, 1)
            nc.gpsimd.affine_select(out=ident[:, :], in_=ident[:, :], compare_op=ALU.not_equal, fill=1.0,
                                    base=0, pattern=[[-1, P]], channel_multiplier=1).then_inc(ident_ready, 1)
            nc.gpsimd.iota(expert_i[:, :], pattern=[[1, EX], [0, RANK]], base=0,
                           channel_multiplier=0).then_inc(iota_ready, 1)

            def centre(first, last):
                for n in range(first, last + 1):
                    centre_ctx(n)

            centre(0, 6)
            pool.wait_ge(peak_ready, 2)
            nc.gpsimd.partition_all_reduce(peak_all[:, :], peak[:, :], P,
                                           bass.bass_isa.ReduceOp.max).then_inc(peak_all_ready, 1)
            centre_ctx(7)
            apply_ar_scale()
            quantise_x(4)
            quantise_x(5)
            centre(8, 15)
            add_corr(0)
            add_corr(1)
            split_ar()
            for k in (0, 1, 3):
                split_w(k)
            add_corr(2)
            for k in range(4, K):
                split_w(k)
            add_corr(3)
            pool.wait_ge(bias_in, 16)
            add_bias(0)
            for t in range(4, T):
                add_corr(t)
            with pool.Fori(1, T) as t:
                add_bias(t)

        @block.scalar
        def _(act):
            def centre_x(t):
                act.wait_ge(x_quantised, t + 1)
                if t >= 2:
                    act.wait_ge(a1_transposed, t - 1)
                nc.scalar.activation(a1[:, t % 2, :], x_u8[:, t % 2, :], ACT.Copy, bias=-CENTRE,
                                     accum_out=rowsum[:, t:t + 1]).then_inc(x_centred, 1)

            def quantise_ctx(n):
                act.wait_ge(*staged(n))
                if n >= 3:
                    act.wait_ge(ctx_centred, n - 2)
                nc.scalar.activation(ctx_u8[:, n % 3, :], stage[:, n % RING, :], ACT.Identity,
                                     bias=prm[:, 3:4], scale=inv_s[:, 2:3]).then_inc(ctx_quantised, 1)

            def make_corr(b):
                act.wait_ge(colsum_done, b + 1)
                nc.scalar.activation(corr[:, b, :].rearrange("p (h n) -> p h n", h=NH),
                                     ps[:, COLSUM_BANKS, :], ACT.Identity,
                                     scale=col_scale).then_inc(corr_ready, 1)

            def split_ar():
                act.wait_ge(ar_scaled, 2)
                nc.scalar.activation(ar_hi[:, :, :].rearrange("p k c -> p (k c)"), y[:, :],
                                     ACT.Copy).then_inc(ar_hi_ready, 1)

            def split_w(k):
                act.wait_ge(*staged(B * K + k))
                nc.scalar.activation(w_hi[:, k, :], stage[:, (B * K + k) % RING, :],
                                     ACT.Copy).then_inc(w_hi_ready, 1)

            def make_y(t, p, first=False):
                act.wait_ge(y_scaled, t + 1)
                if first:
                    act.wait_ge(ar_lo_ready, 1)
                else:
                    act.wait_ge(y_transposed, t)
                nc.scalar.activation(y[:, 0:D], xs[:, t, :], ACT.Identity, bias=y_bias[:, p:p + 1],
                                     scale=y_scale[:, p:p + 1]).then_inc(y_ready, 1)

            def split_yt(t, p, banks, first=False):
                act.wait_ge(y_transposed, t + 1)
                if first:
                    for h, ready in ((0, first_half_hi), (1, yt_hi_ready)):
                        half = yt_hi[:, p, h * K // 2:(h + 1) * K // 2, :]
                        nc.scalar.activation(half.rearrange("p k c -> p (k c)"), ps[:, banks.start + h, :],
                                             ACT.Copy).then_inc(ready, 1)
                else:
                    nc.scalar.activation(yt_hi[:, p, :, :].rearrange("p (h k) c -> p h (k c)", h=2),
                                         ps[:, banks, :], ACT.Copy).then_inc(yt_hi_ready, 1)
                act.wait_ge(yt_hi_ready, t + 1)
                nc.scalar.activation(yt_hi16[:, :, :], yt_hi[:, p, :, :].bitcast(F32), ACT.Copy,
                                     scale=Y_SCALE).then_inc(yt_hi16_ready, 1)

            def gate_weight(t):
                act.wait_ge(gate_diff, t + 1)
                nc.scalar.activation(gate[:, 1:2], gate[:, 0:1], ACT.Exp,
                                     scale=ar_undo[:, 1:2]).then_inc(gate_exp, 1)

            def split_hct(t):
                act.wait_ge(hc_transposed, t + 1)
                nc.scalar.activation(hct_hi[:, :], ps[:, AR_BANK, HCT], ACT.Copy).then_inc(hct_hi_ready, 1)

            act.wait_ge(ones_ready, 1)
            nc.scalar.activation(gate[:, 0:1], ones16[:, 0:1], ACT.Copy)
            act.wait_ge(consts_ready, 1)
            act.wait_ge(quant_in, 16)
            def quantise(first, last):
                for n in range(first, last + 1):
                    quantise_ctx(n)

            quantise(0, 1)
            centre_x(0)
            centre_x(1)
            quantise(2, 6)
            centre_x(2)
            centre_x(3)
            quantise_ctx(7)
            make_corr(0)
            quantise_ctx(8)
            quantise_ctx(9)
            split_ar()
            centre_x(4)
            centre_x(5)
            quantise(10, 15)
            centre_x(6)
            centre_x(7)
            for k in range(3):
                split_w(k)
            make_corr(1)
            make_y(0, 0, first=True)
            split_w(3)
            split_yt(0, 0, yt_banks(0), first=True)
            act.wait_ge(b_in, 16)
            nc.scalar.activation(b_hi[:, :], bias_sb[:, :], ACT.Copy).then_inc(b_hi_ready, 1)
            split_w(4)
            split_w(5)
            gate_weight(0)
            make_y(1, 1)
            split_w(6)
            split_hct(0)
            split_w(7)
            split_yt(1, 1, yt_banks(1))

            def tile(t, p):
                make_y(t + 1, 1 - p)
                gate_weight(t)
                split_hct(t)
                split_yt(t + 1, 1 - p, yt_banks(1))

            with act.Fori(0, (T - 2) // 2) as i:
                tile(2 * i + 1, 1)
                tile(2 * i + 2, 0)
            gate_weight(T - 1)
            split_hct(T - 1)

        @block.vector
        def _(dve):
            steps = [0]

            def then(ins):
                steps[0] += 1
                ins.then_inc(vec_step, 1)
                dve.wait_ge(vec_step, steps[0])

            LN_LINKS = 13

            def statistics(t, p):
                nc.vector.bn_stats(bn[:, p, 0, :], xs[:, t, 0:H])
                return nc.vector.bn_stats(bn[:, p, 1, :], xs[:, t, H:D])

            def layernorm_steps(p, n, link):
                nc.vector.memset(wait_pad[:, :], 0.0)
                for j in range(n):
                    last = nc.vector.bn_aggr(mv[:, p + j, :], bn[:, p + j, :, :].rearrange("p a b -> p (a b)"))
                link(last)
                var = mv[:, p:p + n, 1]
                half, v, g, f, r = (rsq[:, i, p:p + n] for i in range(5))
                nc.vector.tensor_scalar(half, var, EPS, 0.5, ALU.add, ALU.mult)
                link(nc.vector.tensor_scalar(v, var, EPS, None, ALU.add))
                link(nc.vector.tensor_scalar(v.bitcast(I32), v.bitcast(I32), 1, None, ALU.logical_shift_right))
                link(nc.vector.tensor_scalar(r.bitcast(I32), v.bitcast(I32), -1.0, RSQRT_SEED,
                                             ALU.mult, ALU.add))
                link(nc.vector.tensor_tensor(g, half, r, ALU.mult))
                link(nc.vector.tensor_tensor(f, g, r, ALU.mult))
                nc.vector.scalar_tensor_tensor(out=g, in0=f, scalar=-1.5, in1=g, op0=ALU.add, op1=ALU.mult)
                link(nc.vector.scalar_tensor_tensor(out=r, in0=f, scalar=-1.5, in1=r, op0=ALU.add, op1=ALU.mult))
                link(nc.vector.tensor_tensor(f, g, r, ALU.mult))
                link(nc.vector.scalar_tensor_tensor(out=r, in0=f, scalar=-1.5, in1=r, op0=ALU.add, op1=ALU.mult))
                link(nc.vector.tensor_tensor(f, r, r, ALU.mult))
                link(nc.vector.tensor_tensor(f, f, half, ALU.mult))
                link(nc.vector.scalar_tensor_tensor(out=r, in0=f, scalar=-1.5, in1=r, op0=ALU.add, op1=ALU.mult))
                return r

            def statistics_x(t):
                dve.wait_ge(x_in[t], 16)
                statistics(t, t % 2).then_inc(x_statistics, 1)

            def scale_x(t):
                dve.wait_ge(x_statistics, t + 2)
                minus_r = layernorm_steps(0, 2, then)
                nc.vector.tensor_scalar(q_scale[:, t:t + 2], minus_r, -1.0, inv_s[:, 0:1], ALU.mult, ALU.mult)
                then(nc.vector.tensor_tensor(rsq[:, 5, :], mv[:, :, 0], minus_r, ALU.mult))
                nc.vector.tensor_scalar(q_bias[:, t:t + 2], rsq[:, 5, :], inv_s[:, 0:1], prm[:, 1:2],
                                        ALU.mult, ALU.add).then_inc(q_scaled, 1)

            def quantise_x(t):
                dve.wait_ge(q_scaled, t // 2 + 1)
                if t >= 2:
                    dve.wait_ge(x_centred, t - 1)
                nc.vector.tensor_scalar(x_u8[:, t % 2, :], xs[:, t, :], q_scale[:, t:t + 1],
                                        q_bias[:, t:t + 1], ALU.mult, ALU.add).then_inc(x_quantised, 1)

            def take_a1t(t):
                dve.wait_ge(a1_transposed, t + 1)
                if t >= 4:
                    dve.wait_ge(stage1_done, t - 3)
                nc.vector.tensor_copy(a1_t[:, t % 4, :, :].rearrange("p k c -> p (k c)"),
                                      ps[:, a1_bank(t), :].bitcast(BF16)).then_inc(a1t_ready, 1)

            def sum_x1(t):
                dve.wait_ge(stage1_done, t + 1)
                dve.wait_ge(x_quantised, t + 1)
                nc.vector.scalar_tensor_tensor(
                    out=xs[:, t, :].rearrange("p (h n) -> p h n", h=NH),
                    in0=ps[:, s1_bank(t):s1_bank(t) + 2, :], scalar=s12,
                    in1=xs[:, t, :].rearrange("p (h n) -> p h n", h=NH),
                    op0=ALU.mult, op1=ALU.add).then_inc(summed, 1)

            def make_row_terms():
                dve.wait_ge(x_centred, T)
                nc.vector.tensor_scalar(row_term[:, :], rowsum[:, :], k_d1, row_scale,
                                        ALU.add, ALU.mult).then_inc(row_ready, 1)

            def scale_y(t, p):
                n = [0]

                def link(ins):
                    n[0] += 1
                    ins.then_inc(ln_step, 1)
                    dve.wait_ge(ln_step, (t - 2) * LN_LINKS + n[0])

                dve.wait_ge(x1_ready, t + 1)
                dve.wait_ge(y_ready, t - 1)
                link(statistics(t, p))
                minus_r = layernorm_steps(p, 1, link)
                assert n[0] == LN_LINKS, n
                nc.vector.tensor_scalar(y_scale[:, p:p + 1], minus_r, -1.0, None, ALU.mult)
                nc.vector.tensor_tensor(y_bias[:, p:p + 1], mv[:, p, 0:1], minus_r,
                                        ALU.mult).then_inc(y_scaled, 1)

            def scale_first_ys():
                dve.wait_ge(x1_ready, 2)
                statistics(0, 0)
                then(statistics(1, 1))
                minus_r = layernorm_steps(0, 2, then)
                nc.vector.tensor_scalar(y_scale[:, :], minus_r, -1.0, None, ALU.mult)
                nc.vector.tensor_tensor(y_bias[:, :], mv[:, :, 0], minus_r, ALU.mult).then_inc(y_scaled, 2)

            def find_peaks():
                dve.wait_ge(ar_in, 16)
                raw = y[:, :].rearrange("p (k c) -> p k c", c=AR)
                nc.vector.tensor_reduce(peak[:, 0:1], raw[:, :, 0:ER], mybir.AxisListType.XY, ALU.max,
                                        apply_absolute_value=True).then_inc(peak_ready, 1)
                nc.vector.tensor_reduce(peak[:, 1:2], raw[:, :, ER:AR], mybir.AxisListType.XY, ALU.max,
                                        apply_absolute_value=True).then_inc(peak_ready, 1)

            def scale_ar():
                dve.wait_ge(peak_all_ready, 1)
                then(nc.vector.tensor_scalar(peak_all[:, :], peak_all[:, :], AR_FLOOR, 1.0 / AR_SCALE,
                                             ALU.max, ALU.mult))
                then(nc.vector.tensor_scalar(peak_all[:, :].bitcast(I32), peak_all[:, :].bitcast(I32),
                                             EXPONENT, None, ALU.bitwise_and))
                nc.vector.tensor_scalar(ar_undo[:, :], peak_all[:, :], 1.0 / Y_SCALE, None, ALU.mult)
                then(nc.vector.reciprocal(ar_scale[:, :], peak_all[:, :]))
                nc.vector.tensor_scalar(den_scale, ar_scale[:, 0:1], Y_SCALE / SCALING, None,
                                        ALU.mult).then_inc(ar_scale_ready, 1)

            def split_w(k):
                dve.wait_ge(w_hi_ready, k + 1)
                nc.vector.tensor_tensor(w_lo[:, k, :], stage[:, (B * K + k) % RING, :],
                                        w_hi[:, k, :].bitcast(F32), ALU.subtract).then_inc(w_lo_ready[k], 1)

            def split_yt(t, p, banks, first=False):
                def halves(a):
                    return a.rearrange("p (h k) c -> p h (k c)", h=2)

                if first:
                    for h, hi_ready, lo_ready in ((0, first_half_hi, first_half_lo), (1, yt_hi_ready, yt_lo_ready)):
                        part = (slice(None), p, slice(h * K // 2, (h + 1) * K // 2))
                        dve.wait_ge(hi_ready, 1)
                        nc.vector.tensor_tensor(yt_lo[part].rearrange("p k c -> p (k c)"),
                                                ps[:, banks.start + h, :],
                                                yt_hi[part].rearrange("p k c -> p (k c)").bitcast(F32),
                                                ALU.subtract).then_inc(lo_ready, 1)
                else:
                    dve.wait_ge(yt_hi_ready, t + 1)
                    nc.vector.tensor_tensor(halves(yt_lo[:, p, :, :]), ps[:, banks, :],
                                            halves(yt_hi[:, p, :, :].bitcast(F32)),
                                            ALU.subtract).then_inc(yt_lo_ready, 1)
                dve.wait_ge(yt_hi16_ready, t + 1)
                nc.vector.scalar_tensor_tensor(out=halves(yt_lo16[:, :, :]), in0=ps[:, banks, :],
                                               scalar=Y_SCALE, in1=halves(yt_hi16[:, :, :]),
                                               op0=ALU.mult, op1=ALU.subtract).then_inc(yt_lo16_ready, 1)

            GATE_LINKS = 8

            def gate_tile(t):
                n = [0]

                def link(ins):
                    n[0] += 1
                    ins.then_inc(gate_step, 1)
                    dve.wait_ge(gate_step, t * GATE_LINKS + n[0])

                logits = ps[:, AR_BANK, ER:AR]
                dve.wait_ge(ar_done, t + 1)
                nc.vector.memset(wait_pad[:, :], 0.0)
                link(nc.vector.max(top[:, :], logits))
                nc.vector.tensor_tensor(gate[:, 0:1], top[:, 1:2], top[:, 0:1], ALU.subtract).then_inc(gate_diff, 1)
                link(nc.vector.max_index(top_i[:, :], top[:, :], logits))
                link(nc.vector.tensor_copy(top_f[:, :], top_i[:, :]))
                dve.wait_ge(gate_exp, t + 1)
                link(nc.vector.tensor_scalar(gate[:, 2:3], gate[:, 1:2], 1.0, den_scale, ALU.add, ALU.mult))
                link(nc.vector.reciprocal(gate[:, 3:4], gate[:, 2:3]))
                link(nc.vector.tensor_scalar(gate[:, 4:5], gate[:, 1:2], gate[:, 3:4], None, ALU.mult))
                nc.vector.tensor_scalar(c1[:, :], expert[:, :], top_f[:, 0:1], gate[:, 3:4],
                                        ALU.is_equal, ALU.mult)
                link(nc.vector.tensor_scalar(c2[:, :], expert[:, :], top_f[:, 1:2], gate[:, 4:5],
                                             ALU.is_equal, ALU.mult))
                link(nc.vector.tensor_tensor(cw[:, :], c1[:, :], c2[:, :], ALU.add))
                nc.vector.tensor_tensor(hc[:, :], ps[:, AR_BANK, 0:ER], cw[:, :],
                                        ALU.mult).then_inc(hc_ready, 1)
                assert n[0] == GATE_LINKS

            def split_hct(t):
                dve.wait_ge(hct_hi_ready, t + 1)
                nc.vector.tensor_tensor(hct_lo[:, :], ps[:, AR_BANK, HCT], hct_hi[:, :].bitcast(F32),
                                        ALU.subtract).then_inc(hct_lo_ready, 1)

            def sum_out(t, p):
                nc.vector.scalar_tensor_tensor(
                    out=xs[:, t, 0:D].rearrange("p (h n) -> p h n", n=H),
                    in0=ps[:, OUT_BANK[p]:OUT_BANK[p] + NH, :],
                    scalar=row_term[:, bass.ds(t, 1)],
                    in1=xs[:, t, 0:D].rearrange("p (h n) -> p h n", n=H),
                    op0=ALU.add, op1=ALU.add).then_inc(summed, 1)

            nc.vector.memset(ones16[:, :], 1.0).then_inc(ones_ready, 1)
            dve.wait_ge(quant_in, 16)
            nc.vector.reciprocal(inv_s[:, 0:1], prm[:, 0:1])
            then(nc.vector.reciprocal(inv_s[:, 2:3], prm[:, 2:3]))
            nc.vector.tensor_tensor(s12, prm[:, 0:1], prm[:, 2:3], ALU.mult)
            nc.vector.tensor_scalar(d1, prm[:, 1:2], -1.0, CENTRE, ALU.mult, ALU.add)
            then(nc.vector.tensor_scalar(d2, prm[:, 3:4], -1.0, CENTRE, ALU.mult, ALU.add))
            nc.vector.tensor_tensor(col_scale, d1, s12, ALU.mult)
            nc.vector.tensor_tensor(row_scale, d2, s12, ALU.mult)
            nc.vector.tensor_scalar(k_d1, d1, float(D), None, ALU.mult).then_inc(consts_ready, 1)
            dve.wait_ge(consts_ready, 1)
            dve.wait_ge(ident_ready, 2)
            nc.vector.tensor_copy(ident16[:, :], ident[:, :]).then_inc(ident16_ready, 1)
            dve.wait_ge(iota_ready, 1)
            then(nc.vector.tensor_copy(expert[:, :], expert_i[:, :]))
            statistics_x(0)
            statistics_x(1)
            scale_x(0)
            quantise_x(0)
            quantise_x(1)
            statistics_x(2)
            take_a1t(0)
            take_a1t(1)
            statistics_x(3)
            scale_x(2)
            quantise_x(2)
            quantise_x(3)
            find_peaks()
            scale_ar()
            take_a1t(2)
            take_a1t(3)
            statistics_x(4)
            statistics_x(5)
            scale_x(4)
            sum_x1(0)
            sum_x1(1)
            statistics_x(6)
            take_a1t(4)
            take_a1t(5)
            statistics_x(7)
            scale_x(6)
            quantise_x(6)
            sum_x1(2)
            quantise_x(7)
            sum_x1(3)
            take_a1t(6)
            take_a1t(7)
            sum_x1(4)
            scale_first_ys()
            sum_x1(5)
            make_row_terms()
            split_w(2)
            split_yt(0, 0, yt_banks(0), first=True)
            dve.wait_ge(b_hi_ready, 1)
            nc.vector.tensor_tensor(b_lo[:, :], bias_sb[:, :], b_hi[:, :].bitcast(F32),
                                    ALU.subtract).then_inc(b_lo_ready, 1)
            sum_x1(6)
            gate_tile(0)
            sum_x1(7)
            split_hct(0)
            scale_y(2, 0)
            dve.wait_ge(row_ready, 1)
            split_yt(1, 1, yt_banks(1))

            def tile(t, p, scale=True, split=True):
                gate_tile(t)
                split_hct(t)
                dve.wait_ge(out_done, t)
                dve.wait_ge(bias_added, t)
                sum_out(t - 1, 1 - p)
                if scale:
                    scale_y(t + 2, p)
                if split:
                    split_yt(t + 1, 1 - p, yt_banks(1))

            with dve.Fori(0, (T - 4) // 2) as i:
                tile(2 * i + 1, 1)
                tile(2 * i + 2, 0)
            tile(T - 3, 1)
            tile(T - 2, 0, scale=False)
            tile(T - 1, 1, scale=False, split=False)
            dve.wait_ge(bias_added, T)
            for start, end in LAST_PIECES:
                dve.wait_ge(out_done, T + start // H)
                nc.vector.scalar_tensor_tensor(
                    out=xs[:, T - 1, start:end], in0=ps[:, OUT_BANK[1] + start // H, start % H:start % H + end - start],
                    scalar=row_term[:, T - 1:T], in1=xs[:, T - 1, start:end],
                    op0=ALU.add, op1=ALU.add).then_inc(summed, 1)

        @block.tensor
        def _(pe):
            def transpose_a1(t):
                pe.wait_ge(x_centred, t + 1)
                if t >= 4:
                    pe.wait_ge(summed, t - 3)
                bank = ps[:, a1_bank(t), :].bitcast(BF16)
                for k in range(K):
                    last = nc.tensor.transpose(bank[:, k * P:(k + 1) * P], a1[:, t % 2, k * P:(k + 1) * P],
                                               ident16[:, :])
                last.then_inc(a1_transposed, 1)

            def column_sums(b, k):
                pe.wait_ge(ctx_centred, b * K + k + 1)
                for h in range(NH):
                    last = nc.tensor.matmul(ps[:, COLSUM_BANKS.start + h, :], ones16[:, 0:P],
                                            a2[:, k, h * H:(h + 1) * H], start=k == 0, stop=k == K - 1)
                if k == K - 1:
                    last.then_inc(colsum_done, 1)

            def product(q, k, t):
                pe.wait_ge(ctx_centred, q // PPB * K + k + 1)
                for h in range(NH):
                    last = nc.tensor.matmul(ps[:, s1_bank(t) + h, :], a1_t[:, t % 4, k, :],
                                            a2[:, k, h * H:(h + 1) * H], start=k == 0, stop=k == K - 1)
                if k == K - 1:
                    last.then_inc(stage1_done, 1)
                return last

            def first_pair(q, between):
                pe.wait_ge(a1t_ready, 2 * q + 2)
                for k in range(K):
                    product(q, k, 2 * q)
                    product(q, k, 2 * q + 1)
                    for step in between.get(k, ()):
                        step()

            def second_pair(q, between):
                ahead = 4
                pe.wait_ge(a1t_ready, 2 * q + 2)
                for k in range(ahead):
                    product(q, k, 2 * q)
                pe.wait_ge(corr_ready, q // PPB + 1)
                for k in range(K):
                    if k >= ahead:
                        product(q, k, 2 * q)
                    last = product(q, k, 2 * q + 1)
                    if k < K - 1:
                        last.then_inc(a2_used, 1)
                    for step in between.get(k, ()):
                        step()
                nc.tensor.ldweights(ident16[:, :]).then_inc(a2_used, 1)

            def transpose_y(t, banks):
                pe.wait_ge(y_ready, t + 1)
                for k in range(K):
                    last = nc.tensor.transpose(ps[:, banks.start + k // 4, (k % 4) * P:(k % 4 + 1) * P],
                                               y[:, k * P:(k + 1) * P], ident[:, :])
                last.then_inc(y_transposed, 1)

            def transpose_hc(t):
                pe.wait_ge(hc_ready, t + 1)
                nc.tensor.transpose(ps[:, AR_BANK, HCT], hc[:, :], ident[:, :]).then_inc(hc_transposed, 1)

            def narrow(t):
                pe.wait_ge(yt_hi16_ready, t + 1)
                dst = ps[:, AR_BANK, 0:AR]
                for k in range(K):
                    nc.tensor.matmul(dst, yt_hi16[:, k, :], ar_hi[:, k, :], start=k == 0, stop=False)
                    nc.tensor.matmul(dst, yt_hi16[:, k, :], ar_lo[:, k, :], start=False, stop=False)
                pe.wait_ge(yt_lo16_ready, t + 1)
                for k in range(K):
                    last = nc.tensor.matmul(dst, yt_lo16[:, k, :], ar_hi[:, k, :], start=False, stop=k == K - 1)
                last.then_inc(ar_done, 1)

            def lora(t, p, halves=range(NH), stop=False):
                pe.wait_ge(hct_lo_ready, t + 1)
                for part, rhs in ((hct_hi, b_hi), (hct_hi, b_lo), (hct_lo, b_hi)):
                    for h in halves:
                        ins = nc.tensor.matmul(ps[:, OUT_BANK[p] + h, :], part[:, :], rhs[:, h * H:(h + 1) * H],
                                               start=False, stop=stop and part is hct_lo)
                if stop:
                    ins.then_inc(out_done, 1)

            def main(t, p, between, first=False):
                out_ps = OUT_BANK[p]
                if first:
                    pe.wait_ge(first_half_lo, 1)
                else:
                    pe.wait_ge(yt_lo_ready, t + 1)
                for k in range(K):
                    if first and k == K // 2:
                        pe.wait_ge(yt_lo_ready, 1)
                    if first:
                        pe.wait_ge(w_lo_ready[k], 1)
                    hi, lo = yt_hi[:, p, k, :], yt_lo[:, p, k, :]
                    start, stop = k == 0, k == K - 1
                    for part, rhs in ((hi, w_hi), (hi, w_lo), (lo, w_hi)):
                        for h in range(NH):
                            ins = nc.tensor.matmul(ps[:, out_ps + h, :], part, rhs[:, k, h * H:(h + 1) * H],
                                                   start=start and part is hi and rhs is w_hi,
                                                   stop=stop and part is lo)
                            if stop and part is lo and h == NH - 1:
                                ins.then_inc(out_done, 1)
                    if k in between:
                        between[k]()

            pe.wait_ge(ones_ready, 1)
            pe.wait_ge(x_in[0], 16)
            for _ in range(WARM_UP):
                nc.tensor.matmul(ps[:, COLSUM_BANKS.start, 0:3 * P], ones16[:, 0:P], ones16[:, :],
                                 start=True, stop=True)
            pe.wait_ge(ident16_ready, 1)
            column_sums(0, 0)
            column_sums(0, 1)
            transpose_a1(0)
            transpose_a1(1)
            first_pair(0, {k: [lambda k=k: column_sums(0, k)] for k in range(2, K)} |
                       {5: [lambda: column_sums(0, 5), lambda: transpose_a1(2), lambda: transpose_a1(3)]})
            second_pair(1, {5: [lambda: transpose_a1(4)], 6: [lambda: transpose_a1(5)]})
            first_pair(2, {6: [lambda: transpose_a1(6)], 7: [lambda: transpose_a1(7)]})
            for k in range(K):
                column_sums(1, k)
            pe.wait_ge(ident_ready, 2)

            def first_y():
                pe.wait_ge(summed, TB + 2)
                transpose_y(0, yt_banks(0))
            second_pair(3, {5: [first_y]})

            def second_y():
                pe.wait_ge(summed, T)
                transpose_y(1, yt_banks(1))


            def first_narrow():
                pe.wait_ge(ar_lo_ready, 1)
                pe.wait_ge(yt_lo16_ready, 1)
                narrow(0)

            main(0, 0, {1: first_narrow, 4: lambda: (transpose_hc(0), second_y()),
                        6: lambda: (pe.wait_ge(b_lo_ready, 1), lora(0, 0))}, first=True)

            def tile(t, p):
                narrow(t)
                pe.wait_ge(summed, T + t - 1)
                main(t, p, {2: lambda: transpose_hc(t), 3: lambda: transpose_y(t + 1, yt_banks(1)),
                            5: lambda: lora(t, p)})

            with pe.Fori(0, (T - 2) // 2) as i:
                tile(2 * i + 1, 1)
                tile(2 * i + 2, 0)
            last, p = T - 1, 1
            narrow(last)
            pe.wait_ge(summed, T + last - 1)
            for h in range(NH):
                for k in range(K):
                    hi, lo = yt_hi[:, p, k, :], yt_lo[:, p, k, :]
                    for part, rhs in ((hi, w_hi), (hi, w_lo), (lo, w_hi)):
                        nc.tensor.matmul(ps[:, OUT_BANK[p] + h, :], part, rhs[:, k, h * H:(h + 1) * H],
                                         start=k == 0 and part is hi and rhs is w_hi, stop=False)
                    if h == 0 and k == 5:
                        transpose_hc(last)
                lora(last, p, [h], stop=True)


def kernel(x, ctx_4096, L0_xattn_x1_scale, L0_xattn_x1_zp, L0_xattn_x2_scale, L0_xattn_x2_zp,
           L0_ffn_W_base, L0_ffn_b_base, L0_ffn_W_router, L0_ffn_A_stack, L0_ffn_B_stack):
    import numpy as np
    import concourse.bacc as bacc
    from concourse.bass_utils import run_bass_kernel_spmd as run

    D = x.shape[-1]
    experts, rank, _ = L0_ffn_A_stack.shape
    ar = np.concatenate([np.reshape(L0_ffn_A_stack, (experts * rank, D)), np.asarray(L0_ffn_W_router)])
    ar = np.transpose(np.reshape(ar.T, (D // P, P, experts * rank + experts)), (1, 0, 2))
    arrays = {
        "x": x, "ctx_kv": ctx_4096,
        "quant": np.concatenate([np.reshape(v, (1,)) for v in (L0_xattn_x1_scale, L0_xattn_x1_zp,
                                                               L0_xattn_x2_scale, L0_xattn_x2_zp)]),
        "w_t": np.transpose(L0_ffn_W_base), "bias": L0_ffn_b_base,
        "ar_t": np.reshape(ar, (P, -1)),
        "b_t": np.reshape(np.transpose(L0_ffn_B_stack, (0, 2, 1)), (experts * rank, D)),
    }
    arrays = {name: np.ascontiguousarray(a) for name, a in arrays.items()}
    nc = bacc.Bacc("TRN2", target_bir_lowering=False, num_devices=1)
    args = {name: nc.dram_tensor(f"in_{name}", a.shape, mybir.dt.from_np(a.dtype), kind="ExternalInput").ap()
            for name, a in arrays.items()}
    args["out"] = nc.dram_tensor("out_dram", x.shape, F32, kind="ExternalOutput").ap()
    xattn_ffn(nc, **args)
    result = run(nc, [{f"in_{name}": a for name, a in arrays.items()}], core_ids=[0])
    return result.results[0]["out_dram"]
```
